# Optimizing a Trainium2 kernel written in Bass

```python
import numpy as np
import jax
import jax.numpy as jnp

def _softmax(x, axis=-1):
    return jax.nn.softmax(x, axis=axis)

def _gelu(x):
    return jax.nn.gelu(x, approximate=True)

def _silu(x):
    return jax.nn.silu(x)

def _sigmoid(x):
    return jax.nn.sigmoid(x)

def _layernorm(x, axis=-1, eps=1e-05):
    m = jnp.mean(x, axis=axis, keepdims=True)
    v = jnp.var(x, axis=axis, keepdims=True)
    return (x - m) / jnp.sqrt(v + eps)

def _scatter_add(tgt, idx, src, axis=0):
    return tgt.at[idx].add(src)

def _segment_sum(src, seg, n):
    return jax.ops.segment_sum(src, seg, n)
kernel_name = 'mk_recurrent_d1_jaxref_r4_872cd1'

def setup_inputs(seed: int=0):
    np.random.seed(seed)
    _w = jnp.asarray

    def _L0_attn_setup():
        import jax, jax.numpy as jnp
        import numpy as np
        MAX_WAVELENGTH = 10000.0
        NEG_INF = -1000000000.0

        def apply_rope(x):
            S, D = (x.shape[1], x.shape[-1])
            inv_freq = 1.0 / MAX_WAVELENGTH ** (jnp.arange(0, D, 2, dtype=jnp.float32) / D)
            t = jnp.arange(S, dtype=jnp.float32)[:, None] * inv_freq[None, :]
            emb = jnp.concatenate([t, t], axis=-1)
            cos = jnp.cos(emb)[None, :, None, :].astype(x.dtype)
            sin = jnp.sin(emb)[None, :, None, :].astype(x.dtype)
            x1, x2 = jnp.split(x, 2, axis=-1)
            rotated = jnp.concatenate([-x2, x1], axis=-1)
            return x * cos + rotated * sin
        key = jax.random.key(seed)
        k1, k2, k3 = jax.random.split(key, 3)
        B, S, dim = (2, 512, 256)
        x = jax.random.normal(k1, (B, S, dim), dtype=jnp.float32)
        w_qkv = jax.random.normal(k2, (dim, 3 * dim), dtype=jnp.float32) * dim ** (-0.5)
        w_proj = jax.random.normal(k3, (dim, dim), dtype=jnp.float32) * dim ** (-0.5)
        b_proj = jnp.zeros((dim,), dtype=jnp.float32)
        return {'x': x, 'w_qkv': w_qkv, 'w_proj': w_proj, 'b_proj': b_proj}
    _L0_attn_in = _L0_attn_setup()

    def _L0_ffn_setup():
        import jax, jax.numpy as jnp
        import numpy as np
        TOP_K = 8
        CAPACITY = 128

        def _silu(x):
            return x * jax.nn.sigmoid(x)
        key = jax.random.key(seed)
        ks = jax.random.split(key, 7)
        B, S, H, E, I, Is = (2, 256, 256, 64, 128, 512)
        s = 0.05
        return {'hidden_states': jax.random.normal(ks[0], (B, S, H), jnp.float32), 'gate_w': jax.random.normal(ks[1], (H, E), jnp.float32) * s, 'shared_gate_w': jax.random.normal(ks[2], (H, 1), jnp.float32) * s, 'shared_gate_up_w': jax.random.normal(ks[3], (H, 2 * Is), jnp.float32) * s, 'shared_down_w': jax.random.normal(ks[4], (Is, H), jnp.float32) * s, 'expert_gate_up_w': jax.random.normal(ks[5], (E, H, 2 * I), jnp.float32) * s, 'expert_down_w': jax.random.normal(ks[6], (E, I, H), jnp.float32) * s}
    _L0_ffn_in = _L0_ffn_setup()
    _d = {'L0_attn_x': _L0_attn_in['x'], 'L0_attn_w_qkv': _L0_attn_in['w_qkv'], 'L0_attn_w_proj': _L0_attn_in['w_proj'], 'L0_attn_b_proj': _L0_attn_in['b_proj'], 'L0_ffn_gate_w': _L0_ffn_in['gate_w'], 'L0_ffn_shared_gate_w': _L0_ffn_in['shared_gate_w'], 'L0_ffn_shared_gate_up_w': _L0_ffn_in['shared_gate_up_w'], 'L0_ffn_shared_down_w': _L0_ffn_in['shared_down_w'], 'L0_ffn_expert_gate_up_w': _L0_ffn_in['expert_gate_up_w'], 'L0_ffn_expert_down_w': _L0_ffn_in['expert_down_w']}
    _x0 = _d['L0_attn_x']
    _d['L0_attn_x'] = jax.random.normal(jax.random.fold_in(jax.random.key(seed), 1), (16, 1024, 256), dtype=_x0.dtype)
    del _x0
    return _d

def reference(L0_attn_x, L0_attn_w_qkv, L0_attn_w_proj, L0_attn_b_proj, L0_ffn_gate_w, L0_ffn_shared_gate_w, L0_ffn_shared_gate_up_w, L0_ffn_shared_down_w, L0_ffn_expert_gate_up_w, L0_ffn_expert_down_w):

    def _L0_attn_ref(x, w_qkv, w_proj, b_proj):
        import jax, jax.numpy as jnp
        import numpy as np
        MAX_WAVELENGTH = 10000.0
        NEG_INF = -1000000000.0

        def apply_rope(x):
            S, D = (x.shape[1], x.shape[-1])
            inv_freq = 1.0 / MAX_WAVELENGTH ** (jnp.arange(0, D, 2, dtype=jnp.float32) / D)
            t = jnp.arange(S, dtype=jnp.float32)[:, None] * inv_freq[None, :]
            emb = jnp.concatenate([t, t], axis=-1)
            cos = jnp.cos(emb)[None, :, None, :].astype(x.dtype)
            sin = jnp.sin(emb)[None, :, None, :].astype(x.dtype)
            x1, x2 = jnp.split(x, 2, axis=-1)
            rotated = jnp.concatenate([-x2, x1], axis=-1)
            return x * cos + rotated * sin
        B, S, dim = x.shape
        heads = 16
        head_dim = dim // heads
        scale = head_dim ** (-0.5)
        qkv = x @ w_qkv
        qkv = qkv.reshape(B, S, 3, heads, head_dim)
        Q, K, V = (qkv[:, :, 0], qkv[:, :, 1], qkv[:, :, 2])
        Q = apply_rope(Q)
        K = apply_rope(K)
        attn = jnp.einsum('bqhd,bkhd->bhqk', Q, K) * scale
        causal = jnp.tril(jnp.ones((S, S), dtype=bool))[None, None]
        attn = jnp.where(causal, attn, jnp.asarray(NEG_INF, attn.dtype))
        attn = jax.nn.softmax(attn, axis=-1)
        out = jnp.einsum('bhqk,bkhd->bqhd', attn, V).reshape(B, S, dim)
        return out @ w_proj + b_proj

    def _L0_ffn_ref(hidden_states, gate_w, shared_gate_w, shared_gate_up_w, shared_down_w, expert_gate_up_w, expert_down_w):
        import jax, jax.numpy as jnp
        import numpy as np
        TOP_K = 8
        CAPACITY = 128

        def _silu(x):
            return x * jax.nn.sigmoid(x)
        B, S, H = hidden_states.shape
        x = hidden_states.reshape(-1, H)
        T = x.shape[0]
        E = gate_w.shape[1]
        Is = shared_gate_up_w.shape[1] // 2
        I = expert_gate_up_w.shape[2] // 2
        gu = x @ shared_gate_up_w
        shared = _silu(gu[:, :Is]) * gu[:, Is:] @ shared_down_w
        shared = shared * jax.nn.sigmoid(x @ shared_gate_w)
        logits = x @ gate_w
        probs = jax.nn.softmax(logits.astype(jnp.float32), axis=-1)
        w, idx = jax.lax.top_k(probs, TOP_K)
        w = (w / jnp.sum(w, axis=-1, keepdims=True)).astype(x.dtype)
        e_flat = idx.reshape(-1)
        w_flat = w.reshape(-1)
        A = e_flat.shape[0]
        tok = jnp.arange(A) // TOP_K
        onehot = jax.nn.one_hot(e_flat, E, dtype=jnp.int32)
        pos = jnp.take_along_axis(jnp.cumsum(onehot, axis=0) - 1, e_flat[:, None], axis=1)[:, 0]
        slot = jnp.minimum(pos, CAPACITY)
        buf = jnp.zeros((E, CAPACITY + 1, H), x.dtype).at[e_flat, slot].set(x[tok])
        gu_e = jnp.einsum('ech,ehf->ecf', buf, expert_gate_up_w)
        act = _silu(gu_e[..., :I]) * gu_e[..., I:]
        out_e = jnp.einsum('eci,eih->ech', act, expert_down_w)
        y = out_e[e_flat, slot] * w_flat[:, None]
        y = jnp.where((pos < CAPACITY)[:, None], y, jnp.zeros_like(y))
        y = y.reshape(T, TOP_K, H).sum(axis=1)
        return (y + shared).reshape(B, S, H)
    x = L0_attn_x
    xn = _layernorm(x, axis=-1)
    s = _L0_attn_ref(xn, L0_attn_w_qkv, L0_attn_w_proj, L0_attn_b_proj)
    g = _silu(_L0_ffn_ref(xn, L0_ffn_gate_w, L0_ffn_shared_gate_w, L0_ffn_shared_gate_up_w, L0_ffn_shared_down_w, L0_ffn_expert_gate_up_w, L0_ffn_expert_down_w))
    x = x + s * g
    return x

_drawn_inputs = setup_inputs


def setup_inputs(seed=0):
    import zlib

    import numpy as np

    out = dict(_drawn_inputs(seed))
    spreads = {'L0_attn_b_proj': (0.0, 0.667)}
    factors = {'L0_attn_w_qkv': 3.863,
     'L0_attn_w_proj': 3.843,
     'L0_ffn_gate_w': 8.0,
     'L0_ffn_shared_gate_w': 8.0,
     'L0_ffn_shared_gate_up_w': 3.039,
     'L0_ffn_shared_down_w': 3.025,
     'L0_ffn_expert_gate_up_w': 8.0,
     'L0_ffn_expert_down_w': 8.0}
    for name, (base, spread) in spreads.items():
        noise = np.random.default_rng([zlib.crc32(name.encode()), seed]).standard_normal(out[name].shape)
        drawn = base * np.exp(spread * noise) if base else spread * noise
        out[name] = jnp.asarray(drawn.astype(out[name].dtype))
    for name, factor in factors.items():
        out[name] = (out[name] * factor).astype(out[name].dtype)
    return out
```

```python
from contextlib import ExitStack

import concourse.bass as bass
import numpy as np
from concourse import mybir

F32 = mybir.dt.float32
BF16 = mybir.dt.bfloat16
I32 = mybir.dt.int32
ACT = mybir.ActivationFunctionType
ALU = mybir.AluOpType
AX_X = mybir.AxisListType.X

P = 128
B, S, D = 16, 1024, 256
TOK = B * S
E, CAP, TOPK = 64, 128, 8
IS, IE = 512, 128
DC = D // P
BLK = 512
BT = BLK // P
NBLK = TOK // BLK
NTILE = TOK // P
EPS = 1e-5
MASKED = -1e30
LOWEST = -3e38


def feed_forward(nc, x, gate_w, shared_gate_w, shared_gu_w, shared_down_w, expert_gu_w, expert_down_w,
                 consts, xnT_dram, y_dram, cum_dram, wts_dram, ends_dram):
    with ExitStack() as ctx:
        def sb(name, shape, dt=F32):
            return ctx.enter_context(nc.sbuf_tensor(name, shape, dt))

        def psum(name, shape):
            return ctx.enter_context(nc.psum_tensor(name, shape, F32))

        def sem(name):
            return ctx.enter_context(nc.semaphore(name))

        w_router = sb("w_router", [P, DC, E + 1])
        w_gu = sb("w_gu", [P, DC, 2 * IS])
        w_down = sb("w_down", [P, IS // P, D])
        ident = sb("ident", [P, P])
        tri_f = sb("tri_f", [P, P])
        tri = sb("tri", [P, P], BF16)
        ones = sb("ones", [P, P], BF16)
        neg_half = sb("neg_half", [P, BT])
        x_t = sb("x_t", [P, 2, BT, D])
        stats = sb("stats", [P, 2, BT, 6])
        meanvar = sb("meanvar", [P, 2, BT, 2])
        var_eps = sb("var_eps", [P, 2, BT])
        rstd = sb("rstd", [P, 2, BT])
        xn = sb("xn", [P, 2, BT, D])
        xnT = sb("xnT", [P, 2, DC, BLK])
        logits = sb("logits", [P, 2, BT, E + 1])
        top = sb("top", [P, 2, BT, TOPK])
        rest = sb("rest", [P, 2, BT, E])
        chosen = sb("chosen", [P, 2, BT, E], BF16)
        shifted = sb("shifted", [P, 2, BT, E])
        expo = sb("expo", [P, 2, BT, E])
        picked = sb("picked", [P, 2, BT, E])
        picked_sum = sb("picked_sum", [P, 2, BT])
        picked_inv = sb("picked_inv", [P, 2, BT])
        wts = sb("wts", [P, 2, BT, E])
        gate_exp = sb("gate_exp", [P, 2, BT])
        gate_den = sb("gate_den", [P, 2, BT])
        gate_sig = sb("gate_sig", [P, 2, BT])
        base = sb("base", [E, 1])
        cum = sb("cum", [E, 2, BLK])
        ends = sb("ends", [E, NTILE])
        silu = sb("silu", [P, 2, BLK])
        act = sb("act", [P, IS // P, BLK])
        y_t = sb("y_t", [P, 2, BT, D])

        ps_td = psum("ps_td", [P, 2, 512])
        ps_router = psum("ps_router", [P, BT, E + 1])
        ps_cum = psum("ps_cum", [E, BLK])
        ps_gu = psum("ps_gu", [P, 2, 2, 512])

        waited = sem("waited")
        weights_in = sem("weights_in")
        consts_in = sem("consts_in")
        setup = sem("setup")
        x_in = [sem("x_in0"), sem("x_in1")]
        stats_done = sem("stats_done")
        var_done = sem("var_done")
        rstd_done = sem("rstd_done")
        stats_step = sem("stats_step")
        xn_done = sem("xn_done")
        transposed = sem("transposed")
        xnT_done = sem("xnT_done")
        xnT_out = [sem("xnT_out0"), sem("xnT_out1")]
        router_done = sem("router_done")
        logits_done = sem("logits_done")
        top_done = sem("top_done")
        rest_done = sem("rest_done")
        chosen_done = sem("chosen_done")
        shifted_done = sem("shifted_done")
        expo_done = sem("expo_done")
        gate_exp_done = sem("gate_exp_done")
        picked_done = sem("picked_done")
        sum_done = sem("sum_done")
        inv_done = sem("inv_done")
        gate_den_done = sem("gate_den_done")
        wts_done = sem("wts_done")
        wts_out = [sem("wts_out0"), sem("wts_out1")]
        gate_done = sem("gate_done")
        counted = sem("counted")
        cum_done = sem("cum_done")
        base_done = sem("base_done")
        ends_done = sem("ends_done")
        cum_out = [sem("cum_out0"), sem("cum_out1")]
        gu_done = sem("gu_done")
        silu_done = sem("silu_done")
        act_done = sem("act_done")
        down_done = sem("down_done")
        y_done = sem("y_done")
        y_out = [sem("y_out0"), sem("y_out1")]
        ends_out = sem("ends_out")

        NJ = IS // P
        x_b = x.rearrange("(n t p) d -> n p t d", t=BT, p=P)
        y_b = y_dram.rearrange("(n t p) d -> n p t d", t=BT, p=P)
        wts_b = wts_dram.rearrange("(n t p) e -> n p t e", t=BT, p=P)

        def per_block(engine, step):
            for u in range(2):
                step(u, u, 0, True)
            with engine.Fori(1, NBLK // 2) as i:
                for u in range(2):
                    step(i * 2 + u, u, i, False)

        with nc.Block() as block:
            @block.sync
            def _(sp):
                sp.dma_start(ident[:, :], consts[:, 0:P]).then_inc(consts_in, 16)
                sp.dma_start(tri_f[:, :], consts[:, P:2 * P]).then_inc(consts_in, 16)
                sp.dma_start(w_router[:, :, 0:E], gate_w.rearrange("(c p) e -> p c e", p=P),
                             allow_slow_non_contiguous=True).then_inc(weights_in, 16)
                sp.dma_start(w_router[:, :, E:E + 1], shared_gate_w.rearrange("(c p) e -> p c e", p=P),
                             allow_slow_non_contiguous=True).then_inc(weights_in, 16)
                sp.dma_start(w_gu[:, :, :], shared_gu_w.rearrange("(c p) f -> p c f", p=P)).then_inc(weights_in, 16)
                sp.dma_start(w_down[:, :, :], shared_down_w.rearrange("(c p) f -> p c f", p=P)).then_inc(weights_in, 16)

                def load(n, u, i, early):
                    if not early:
                        sp.wait_ge(xn_done, (n - 1) * BT)
                    sp.dma_start(x_t[:, u], x_b[n]).then_inc(x_in[u], 16)
                per_block(sp, load)

            @block.gpsimd
            def _(pool):
                pool.memset(neg_half[:, :], -0.5).then_inc(setup, 1)
                pool.memset(ones[:, :], 1.0).then_inc(setup, 1)
                pool.wait_ge(setup, 2)

                def finish(n, u, i, early):
                    if not early:
                        pool.wait_ge(xn_done, (n - 1) * BT)
                    pool.wait_ge(var_done, n + 1)
                    pool.tensor_tensor(rstd[:, u], var_eps[:, u], neg_half[:, :], ALU.pow).then_inc(rstd_done, 1)
                    pool.wait_ge(wts_done, n + 1)
                    pool.sem_inc(waited, 1)
                    pool.dma_start(wts_b[n], wts[:, u]).then_inc(wts_out[u], 16)
                    pool.wait_ge(cum_done, n + 1)
                    pool.sem_inc(waited, 1)
                    pool.dma_start(cum_dram[:, bass.ds(n * BLK, BLK)], cum[:, u]).then_inc(cum_out[u], 16)
                    pool.wait_ge(y_done, (n + 1) * BT)
                    pool.sem_inc(waited, 1)
                    pool.dma_start(y_b[n], y_t[:, u]).then_inc(y_out[u], 16)
                per_block(pool, finish)
                pool.wait_ge(ends_done, NBLK)
                pool.dma_start(ends_dram, ends[:, :]).then_inc(ends_out, 16)
                pool.wait_ge(ends_out, 16)
                for u in range(2):
                    pool.wait_ge(wts_out[u], 16 * (NBLK // 2))
                    pool.wait_ge(cum_out[u], 16 * (NBLK // 2))
                    pool.wait_ge(y_out[u], 16 * (NBLK // 2))

            @block.scalar
            def _(act_e):
                def work(n, u, i, early):
                    if not early:
                        act_e.wait_ge(xnT_out[u], i * 16)
                        act_e.wait_ge(gu_done, (n - 1) * NJ)
                        act_e.wait_ge(router_done, n - 1)
                    for c in range(DC):
                        act_e.wait_ge(transposed, n * DC + (c + 1))
                        act_e.activation(xnT[:, u, c, :], ps_td[:, c, :], ACT.Copy).then_inc(xnT_done, 1)
                    act_e.wait_ge(xnT_done, (n + 1) * DC)
                    act_e.dma_start(xnT_dram[n], xnT[:, u]).then_inc(xnT_out[u], 16)
                    if not early:
                        act_e.wait_ge(picked_done, n - 1)
                        act_e.wait_ge(gate_den_done, n - 1)
                    act_e.wait_ge(shifted_done, n + 1)
                    act_e.activation(expo[:, u], shifted[:, u], ACT.Exp).then_inc(expo_done, 1)
                    act_e.activation(gate_exp[:, u], logits[:, u, :, E], ACT.Exp, scale=-1.0).then_inc(gate_exp_done, 1)
                    for j in range(NJ):
                        if not (early and u == 0 and j < 2):
                            act_e.wait_ge(act_done, n * NJ + (j - 1))
                        act_e.wait_ge(gu_done, n * NJ + (j + 1))
                        act_e.activation(silu[:, j % 2, :], ps_gu[:, j % 2, 0, :], ACT.Silu).then_inc(silu_done, 1)
                    if not early:
                        act_e.wait_ge(y_out[u], i * 16)
                    act_e.wait_ge(gate_done, n + 1)
                    for t in range(BT):
                        if t % 2 == 0:
                            act_e.wait_ge(down_done, n * BT + (t + 2))
                        act_e.activation(y_t[:, u, t, :], ps_td[:, t // 2, (t % 2) * D:(t % 2 + 1) * D], ACT.Copy,
                                         scale=gate_sig[:, u, t:t + 1]).then_inc(y_done, 1)
                per_block(act_e, work)
                for u in range(2):
                    act_e.wait_ge(xnT_out[u], 16 * (NBLK // 2))

            @block.vector
            def _(dve):
                dve.wait_ge(consts_in, 32)
                dve.tensor_copy(tri[:, :], tri_f[:, :]).then_inc(setup, 1)
                dve.memset(base[:, :], 0.0).then_inc(base_done, 1)

                def work(n, u, i, early):
                    dve.wait_ge(x_in[u], i * 16 + 16)
                    for t in range(BT):
                        if not early and t == 0:
                            dve.wait_ge(stats_step, (n - 1) * BT)
                        dve.bn_stats(stats[:, u, t, :], x_t[:, u, t, :]).then_inc(stats_done, 1)
                    if not early:
                        dve.wait_ge(transposed, (n - 1) * DC)
                        dve.wait_ge(xn_done, (n - 1) * BT)
                    for t in range(BT):
                        dve.wait_ge(stats_done, n * BT + (t + 1))
                        dve.sem_inc(waited, 1)
                        dve.bn_aggr(meanvar[:, u, t, :], stats[:, u, t, :]).then_inc(stats_step, 1)
                    dve.wait_ge(stats_step, (n + 1) * BT)
                    dve.tensor_scalar(var_eps[:, u], meanvar[:, u, :, 1], EPS, None, ALU.add).then_inc(var_done, 1)
                    dve.wait_ge(rstd_done, n + 1)
                    for t in range(BT):
                        dve.tensor_scalar(xn[:, u, t, :], x_t[:, u, t, :], meanvar[:, u, t, 0:1],
                                          rstd[:, u, t:t + 1], ALU.subtract, ALU.mult).then_inc(xn_done, 1)
                    if not early:
                        dve.wait_ge(gate_exp_done, n - 1)
                    dve.wait_ge(router_done, n + 1)
                    dve.tensor_copy(logits[:, u], ps_router[:, :, :]).then_inc(logits_done, 1)
                    dve.wait_ge(logits_done, n + 1)
                    dve.sem_inc(waited, 1)
                    for t in range(BT):
                        dve.max(top[:, u, t, :], logits[:, u, t, 0:E]).then_inc(top_done, 1)
                    for t in range(BT):
                        dve.wait_ge(top_done, n * BT + (t + 1))
                        dve.sem_inc(waited, 1)
                        dve.match_replace(rest[:, u, t, :], top[:, u, t, :], logits[:, u, t, 0:E], LOWEST).then_inc(rest_done, 1)
                    if not early:
                        dve.wait_ge(counted, n - 1)
                    dve.wait_ge(rest_done, (n + 1) * BT)
                    dve.tensor_tensor(chosen[:, u], rest[:, u], logits[:, u, :, 0:E], ALU.not_equal).then_inc(chosen_done, 1)
                    dve.tensor_tensor(shifted[:, u], logits[:, u, :, 0:E],
                                      top[:, u, :, 0:1].to_broadcast([P, BT, E]), ALU.subtract).then_inc(shifted_done, 1)

                    def gated(j):
                        if not (early and u == 0) and j == 0:
                            dve.wait_ge(down_done, n * BT)
                        dve.wait_ge(silu_done, n * NJ + (j + 1))
                        dve.tensor_tensor(act[:, j, :], silu[:, j % 2, :], ps_gu[:, j % 2, 1, :], ALU.mult).then_inc(act_done, 1)

                    gated(0)
                    dve.wait_ge(expo_done, n + 1)
                    dve.tensor_tensor(picked[:, u], expo[:, u], chosen[:, u], ALU.mult).then_inc(picked_done, 1)
                    dve.wait_ge(gate_exp_done, n + 1)
                    dve.tensor_scalar(gate_den[:, u], gate_exp[:, u], 1.0, None, ALU.add).then_inc(gate_den_done, 1)
                    dve.wait_ge(picked_done, n + 1)
                    dve.tensor_reduce(picked_sum[:, u], picked[:, u], AX_X, ALU.add).then_inc(sum_done, 1)
                    if not early:
                        dve.wait_ge(y_done, (n - 1) * BT)
                    dve.wait_ge(gate_den_done, n + 1)
                    dve.reciprocal(gate_sig[:, u], gate_den[:, u]).then_inc(gate_done, 1)
                    dve.wait_ge(sum_done, n + 1)
                    dve.reciprocal(picked_inv[:, u], picked_sum[:, u]).then_inc(inv_done, 1)
                    gated(1)
                    if not early:
                        dve.wait_ge(wts_out[u], i * 16)
                    dve.wait_ge(inv_done, n + 1)
                    dve.tensor_tensor(wts[:, u], picked[:, u],
                                      picked_inv[:, u].unsqueeze(2).to_broadcast([P, BT, E]), ALU.mult).then_inc(wts_done, 1)
                    gated(2)
                    if not early:
                        dve.wait_ge(cum_out[u], i * 16)
                    dve.wait_ge(counted, n + 1)
                    dve.wait_ge(base_done, n + 1)
                    dve.tensor_scalar(cum[:, u], ps_cum[:, :], base[:, 0:1], None, ALU.add).then_inc(cum_done, 1)
                    gated(3)
                    dve.wait_ge(cum_done, n + 1)
                    dve.tensor_copy(base[:, :], cum[:, u, BLK - 1:BLK]).then_inc(base_done, 1)
                    dve.tensor_copy(ends[:, bass.ds(n * BT, BT)], cum[:, u, P - 1:BLK:P]).then_inc(ends_done, 1)
                per_block(dve, work)

            @block.tensor
            def _(pe):
                pe.wait_ge(setup, 3)
                pe.wait_ge(consts_in, 32)
                pe.wait_ge(weights_in, 64)

                def work(n, u, i, early):
                    if not (early and u == 0):
                        pe.wait_ge(y_done, n * BT)
                    pe.wait_ge(xn_done, (n + 1) * BT)
                    for c in range(DC):
                        for t in range(BT):
                            last = pe.transpose(ps_td[:, c, t * P:(t + 1) * P], xn[:, u, t, c * P:(c + 1) * P], ident[:, :])
                        last.then_inc(transposed, 1)
                    if not (early and u == 0):
                        pe.wait_ge(logits_done, n)
                    pe.wait_ge(xnT_done, (n + 1) * DC)
                    for t in range(BT):
                        for c in range(DC):
                            last = pe.matmul(ps_router[:, t, :], xnT[:, u, c, t * P:(t + 1) * P], w_router[:, c, :],
                                             start=(c == 0), stop=(c == DC - 1))
                    last.then_inc(router_done, 1)
                    for j in range(NJ):
                        if not (early and u == 0 and j < 2):
                            pe.wait_ge(act_done, n * NJ + (j - 1))
                        for k in range(2):
                            for c in range(DC):
                                f = k * IS + j * P
                                last = pe.matmul(ps_gu[:, j % 2, k, :], w_gu[:, c, f:f + P], xnT[:, u, c, :],
                                                 start=(c == 0), stop=(c == DC - 1))
                        last.then_inc(gu_done, 1)
                    if not (early and u == 0):
                        pe.wait_ge(cum_done, n)
                    pe.wait_ge(chosen_done, n + 1)
                    for t in range(BT):
                        for before in range(t):
                            pe.matmul(ps_cum[:, t * P:(t + 1) * P], chosen[:, u, before, :], ones[:, :],
                                      start=(before == 0), stop=False)
                        last = pe.matmul(ps_cum[:, t * P:(t + 1) * P], chosen[:, u, t, :], tri[:, :],
                                         start=(t == 0), stop=True)
                    last.then_inc(counted, 1)
                    pe.wait_ge(act_done, (n + 1) * NJ)
                    for t in range(BT):
                        for j in range(NJ):
                            last = pe.matmul(ps_td[:, t // 2, (t % 2) * D:(t % 2 + 1) * D], act[:, j, t * P:(t + 1) * P],
                                             w_down[:, j, :], start=(j == 0), stop=(j == NJ - 1))
                        last.then_inc(down_done, 1)
                per_block(pe, work)


NRING = 4


def experts(nc, x, expert_gu_w, expert_down_w, consts, y_dram, cum_dram, wts_dram, ends_dram):
    with ExitStack() as ctx:
        def sb(name, shape, dt=F32):
            return ctx.enter_context(nc.sbuf_tensor(name, shape, dt))

        def psum(name, shape):
            return ctx.enter_context(nc.psum_tensor(name, shape, F32))

        def sem(name):
            return ctx.enter_context(nc.semaphore(name))

        ident = sb("e_ident", [P, P])
        slot = sb("slot", [P, 2])
        row0 = sb("row0", [P, E])
        number = sb("number", [P, E])
        counts = sb("counts", [P, E, P])
        at_most = sb("at_most", [P, E, P])
        tiles = sb("tiles", [P, E])
        tile_c = sb("tile_c", [P, E])
        rowf = sb("rowf", [P, E])
        rows = sb("rows", [P, E], I32)
        within = sb("within", [P, E])
        tokf = sb("tokf", [P, E])
        tok_all = sb("tok_all", [P, E], I32)
        tok_ok = sb("tok_ok", [P, E])
        toks = sb("toks", [P, E], I32)
        wrowf = sb("wrowf", [P, E])
        wrows = sb("wrows", [P, E], I32)
        w_slot = sb("w_slot", [P, E])
        neg_half = sb("e_neg_half", [P, 1])

        w_gu = sb("e_w_gu", [P, NRING, DC, 2 * IE])
        w_down = sb("e_w_down", [P, NRING, D])
        xg = sb("xg", [P, NRING, D])
        stats = sb("e_stats", [P, NRING, 6])
        meanvar = sb("e_meanvar", [P, NRING, 2])
        var_eps = sb("e_var_eps", [P, NRING, 1])
        rstd = sb("e_rstd", [P, NRING, 1])
        xn = sb("e_xn", [P, NRING, D])
        xT = sb("e_xT", [P, NRING, DC, P])
        silu = sb("e_silu", [P, NRING, P])
        act = sb("e_act", [P, NRING, P])
        y_e = sb("y_e", [P, NRING, D])

        ps_t = psum("ps_t", [P, 2, 512])
        ps_gu = psum("e_ps_gu", [P, 2, 512])
        ps_y = psum("ps_y", [P, 2, 512])

        waited = sem("e_waited")
        consts_in = sem("e_consts_in")
        neg_half_set = sem("neg_half_set")
        ends_in = sem("ends_in")
        compared = sem("compared")
        tiles_done = sem("tiles_done")
        tile_c_done = sem("tile_c_done")
        rowf_done = sem("rowf_done")
        rows_done = sem("rows_done")
        counts_in = sem("counts_in")
        within_done = sem("within_done")
        tokf_done = sem("tokf_done")
        tok_ok_done = sem("tok_ok_done")
        toks_done = sem("toks_done")
        wrowf_done = sem("wrowf_done")
        wrows_done = sem("wrows_done")
        w_slot_in = sem("w_slot_in")
        w_in = [sem(f"e_w_in{r}") for r in range(NRING)]
        x_in = [sem(f"e_x_in{r}") for r in range(NRING)]
        stats_done = sem("e_stats_done")
        aggr_done = sem("e_aggr_done")
        var_done = sem("e_var_done")
        rstd_done = sem("e_rstd_done")
        xn_done = sem("e_xn_done")
        transposed = sem("e_transposed")
        xT_done = sem("e_xT_done")
        gu_done = sem("e_gu_done")
        silu_done = sem("e_silu_done")
        act_done = sem("e_act_done")
        down_done = sem("e_down_done")
        y_done = sem("e_y_done")
        added = sem("added")

        count_rows = cum_dram.rearrange("e (t p) -> (e t) p", p=P)
        w_cells = wts_dram.rearrange("t (e o) -> (t e) o", o=1)
        gu_e = expert_gu_w.rearrange("e (c p) f -> e p c f", p=P)

        def per_expert(engine, step):
            for r in range(NRING):
                step(r, r, 0, True)
            with engine.Fori(1, E // NRING) as i:
                for r in range(NRING):
                    step(i * NRING + r, r, i, False)

        with nc.Block() as block:
            @block.sync
            def _(sp):
                sp.dma_start(ident[:, :], consts[:, 0:P]).then_inc(consts_in, 16)
                sp.dma_start(slot[:, :], consts[:, 2 * P:2 * P + 2]).then_inc(consts_in, 16)
                sp.dma_start(row0[:, :], consts[:, 3 * P:3 * P + E]).then_inc(consts_in, 16)
                sp.dma_start(number[:, :], consts[:, 3 * P + E:3 * P + 2 * E]).then_inc(consts_in, 16)
                sp.dma_start(counts[:, :, :].rearrange("p e t -> p (e t)"),
                             ends_dram.rearrange("e (t o) -> o (e t)", o=1).partition_broadcast(P)).then_inc(ends_in, 16)

                def load(e, r, i, early):
                    if not early:
                        sp.wait_ge(down_done, e - (NRING - 1))
                    sp.dma_start(w_gu[:, r], gu_e[e]).then_inc(w_in[r], 16)
                    sp.dma_start(w_down[:, r], expert_down_w[e]).then_inc(w_in[r], 16)
                per_expert(sp, load)

            @block.gpsimd
            def _(pool):
                pool.memset(neg_half[:, :], -0.5).then_inc(neg_half_set, 1)
                pool.wait_ge(neg_half_set, 1)
                pool.wait_ge(rows_done, 1)
                for e in range(E):
                    pool.indirect_dma_start(counts[:, e, :], None, count_rows,
                                            bass.IndirectOffsetOnAxis(rows[:, e:e + 1], 0)).then_inc(counts_in, 16)

                def gather(e):
                    r = e % NRING
                    if e >= NRING:
                        pool.wait_ge(xn_done, e - NRING + 1)
                    pool.indirect_dma_start(xg[:, r, :], None, x,
                                            bass.IndirectOffsetOnAxis(toks[:, e:e + 1], 0)).then_inc(x_in[r], 16)

                pool.wait_ge(toks_done, 1)
                gather(0)
                gather(1)
                pool.wait_ge(wrows_done, 1)
                for e in range(E):
                    pool.indirect_dma_start(w_slot[:, e:e + 1], None, w_cells,
                                            bass.IndirectOffsetOnAxis(wrows[:, e:e + 1], 0)).then_inc(w_slot_in, 16)

                def scatter(e):
                    if e >= 1:
                        pool.wait_ge(added, 16 * e)
                    pool.wait_ge(y_done, e + 1)
                    pool.indirect_dma_start(y_dram, bass.IndirectOffsetOnAxis(tok_all[:, e:e + 1], 0), y_e[:, e % NRING, :],
                                            None, bounds_check=TOK - 1, oob_is_err=False,
                                            compute_op=ALU.add).then_inc(added, 16)

                for e in range(E):
                    r = e % NRING
                    if e + 2 < E:
                        gather(e + 2)
                    pool.wait_ge(var_done, e + 1)
                    pool.tensor_tensor(rstd[:, r], var_eps[:, r], neg_half[:, :], ALU.pow).then_inc(rstd_done, 1)
                    if e >= 1:
                        scatter(e - 1)
                scatter(E - 1)
                pool.wait_ge(added, 16 * E)

            @block.scalar
            def _(act_e):
                def work(e, r, i, early):
                    if not early:
                        act_e.wait_ge(gu_done, e - (NRING - 1))
                    act_e.wait_ge(transposed, e + 1)
                    act_e.activation(xT[:, r].rearrange("p c t -> p (c t)"), ps_t[:, r % 2, 0:DC * P], ACT.Copy).then_inc(xT_done, 1)
                    if not early:
                        act_e.wait_ge(act_done, e - (NRING - 1))
                    act_e.wait_ge(gu_done, e + 1)
                    act_e.activation(silu[:, r], ps_gu[:, r % 2, 0:P], ACT.Silu).then_inc(silu_done, 1)
                per_expert(act_e, work)

            @block.vector
            def _(dve):
                dve.wait_ge(consts_in, 64)
                dve.wait_ge(ends_in, 16)
                both = "p e t -> p (e t)"
                dve.tensor_scalar(at_most[:, :, :].rearrange(both), counts[:, :, :].rearrange(both), slot[:, 0:1], None,
                                  ALU.is_le).then_inc(compared, 1)
                dve.wait_ge(compared, 1)
                dve.tensor_reduce(tiles[:, :], at_most[:, :, :], AX_X, ALU.add).then_inc(tiles_done, 1)
                dve.wait_ge(tiles_done, 1)
                dve.tensor_scalar(tile_c[:, :], tiles[:, :], float(NTILE - 1), None, ALU.min).then_inc(tile_c_done, 1)
                dve.wait_ge(tile_c_done, 1)
                dve.tensor_tensor(rowf[:, :], tile_c[:, :], row0[:, :], ALU.add).then_inc(rowf_done, 1)
                dve.wait_ge(rowf_done, 1)
                dve.tensor_copy(rows[:, :], rowf[:, :]).then_inc(rows_done, 1)
                dve.wait_ge(counts_in, 16 * E)
                dve.tensor_scalar(at_most[:, :, :].rearrange(both), counts[:, :, :].rearrange(both), slot[:, 0:1], None,
                                  ALU.is_le).then_inc(compared, 1)
                dve.wait_ge(compared, 2)
                dve.tensor_reduce(within[:, :], at_most[:, :, :], AX_X, ALU.add).then_inc(within_done, 1)
                dve.wait_ge(within_done, 1)
                dve.scalar_tensor_tensor(out=tokf[:, :], in0=tile_c[:, :], scalar=float(P), in1=within[:, :],
                                         op0=ALU.mult, op1=ALU.add).then_inc(tokf_done, 1)
                dve.wait_ge(tokf_done, 1)
                dve.tensor_copy(tok_all[:, :], tokf[:, :])
                dve.tensor_scalar(tok_ok[:, :], tokf[:, :], float(TOK - 1), None, ALU.min).then_inc(tok_ok_done, 1)
                dve.wait_ge(tok_ok_done, 1)
                dve.tensor_copy(toks[:, :], tok_ok[:, :]).then_inc(toks_done, 1)
                dve.scalar_tensor_tensor(out=wrowf[:, :], in0=tok_ok[:, :], scalar=float(E), in1=number[:, :],
                                         op0=ALU.mult, op1=ALU.add).then_inc(wrowf_done, 1)
                dve.wait_ge(wrowf_done, 1)
                dve.tensor_copy(wrows[:, :], wrowf[:, :]).then_inc(wrows_done, 1)
                dve.wait_ge(w_slot_in, 16 * E)

                def work(e, r, i, early):
                    if not early:
                        dve.wait_ge(aggr_done, e - (NRING - 1))
                    dve.wait_ge(x_in[r], i * 16 + 16)
                    dve.bn_stats(stats[:, r], xg[:, r]).then_inc(stats_done, 1)
                    if not early:
                        dve.wait_ge(xn_done, e - (NRING - 1))
                    dve.wait_ge(stats_done, e + 1)
                    dve.sem_inc(waited, 1)
                    dve.bn_aggr(meanvar[:, r], stats[:, r]).then_inc(aggr_done, 1)
                    dve.wait_ge(aggr_done, e + 1)
                    dve.tensor_scalar(var_eps[:, r], meanvar[:, r, 1:2], EPS, None, ALU.add).then_inc(var_done, 1)
                    if not early:
                        dve.wait_ge(transposed, e - (NRING - 1))
                    dve.wait_ge(rstd_done, e + 1)
                    dve.tensor_scalar(xn[:, r], xg[:, r], meanvar[:, r, 0:1], rstd[:, r], ALU.subtract,
                                      ALU.mult).then_inc(xn_done, 1)
                    if not early:
                        dve.wait_ge(down_done, e - (NRING - 1))
                    dve.wait_ge(silu_done, e + 1)
                    dve.tensor_tensor(act[:, r], silu[:, r], ps_gu[:, r % 2, P:2 * P], ALU.mult).then_inc(act_done, 1)

                def weigh(e, r, early):
                    if not early:
                        dve.wait_ge(added, (e - (NRING - 1)) * 16)
                    dve.wait_ge(down_done, e + 1)
                    dve.tensor_scalar(y_e[:, r], ps_y[:, r % 2, 0:D], w_slot[:, bass.ds(e, 1)],
                                      None, ALU.mult).then_inc(y_done, 1)

                for r in range(NRING):
                    work(r, r, 0, True)
                    if r > 0:
                        weigh(r - 1, r - 1, True)
                with dve.Fori(1, E // NRING) as i:
                    for r in range(NRING):
                        work(i * NRING + r, r, i, False)
                        weigh(i * NRING + (r - 1), (r - 1) % NRING, False)
                weigh(E - 1, NRING - 1, False)

            @block.tensor
            def _(pe):
                pe.wait_ge(consts_in, 64)

                def up(e, r, i, early):
                    if not (early and r < 2):
                        pe.wait_ge(xT_done, e - 1)
                    pe.wait_ge(xn_done, e + 1)
                    for c in range(DC):
                        last = pe.transpose(ps_t[:, r % 2, c * P:(c + 1) * P], xn[:, r, c * P:(c + 1) * P], ident[:, :])
                    last.then_inc(transposed, 1)
                    if not (early and r < 2):
                        pe.wait_ge(act_done, e - 1)
                    pe.wait_ge(w_in[r], i * 32 + 32)
                    pe.wait_ge(xT_done, e + 1)
                    for k in range(2):
                        for c in range(DC):
                            last = pe.matmul(ps_gu[:, r % 2, k * P:(k + 1) * P], w_gu[:, r, c, k * IE:(k + 1) * IE],
                                             xT[:, r, c, :], start=(c == 0), stop=(c == DC - 1))
                    last.then_inc(gu_done, 1)

                def down(e, r, early):
                    if not (early and r < 2):
                        pe.wait_ge(y_done, e - 1)
                    pe.wait_ge(act_done, e + 1)
                    pe.matmul(ps_y[:, r % 2, 0:D], act[:, r], w_down[:, r], start=True, stop=True).then_inc(down_done, 1)

                for r in range(NRING):
                    up(r, r, 0, True)
                    if r > 0:
                        down(r - 1, r - 1, True)
                with pe.Fori(1, E // NRING) as i:
                    for r in range(NRING):
                        up(i * NRING + r, r, i, False)
                        down(i * NRING + (r - 1), (r - 1) % NRING, False)
                down(E - 1, NRING - 1, False)


H, HD = 16, 16
GH = 4
NG = H // GH
GD = GH * HD
QT = S // P
HALF = 512
TERMS_Q = (0, 1, 0, 2, 0, 1)
TERMS_K = (0, 0, 1, 0, 2, 1)
NT = len(TERMS_Q) * HD
NPART = 3
UNITS = [(0, kt) for kt in (0, 3, 2, 1)] + [(1, kt) for kt in (0, 7, 6, 5, 4, 1, 2, 3)]
CHUNKS = [(qt, kh) for qt in range(QT) for kh in range(qt // 4 + 1)]
NU = len(UNITS)
NCH = GH * len(CHUNKS)
AHEAD = 3
UNIT_CHUNKS = (8, 3, 6, 4, 9, 4, 4, 5, 5)
TURN_UNIT = 9
POOL_TERMS = (5,)


def attention(nc, x, w_qkv, w_proj, b_proj, consts, rope, xnT_dram, y_dram, out):
    with ExitStack() as ctx:
        def sb(name, shape, dt=F32):
            return ctx.enter_context(nc.sbuf_tensor(name, shape, dt))

        def psum(name, shape, dt=F32):
            return ctx.enter_context(nc.psum_tensor(name, shape, dt))

        def sem(name):
            return ctx.enter_context(nc.semaphore("a_" + name))

        const_f = sb("const_f", [P, 3, P])
        ident = sb("ident_bf", [P, P], BF16)
        mask_qk = sb("mask_qk", [P, P], BF16)
        mask_kq = sb("mask_kq", [P, P], BF16)
        cos = sb("cos", [P, S])
        sin = sb("sin", [P, S])
        w_qk = sb("w_qk", [P, DC, NG, 2 * GD])
        w_v = sb("w_v", [P, DC, D])
        w_o = sb("w_o", [P, DC, D])
        bias = sb("bias", [P, 1, D])
        xT = sb("xT", [P, 2, DC, BLK])
        qk = sb("qk", [P, 2, HALF])
        rot = sb("rot", [P, 2, HALF])
        qc = sb("qc", [P, 2, HALF])
        rs = sb("rs", [P, 2, HALF])
        parts = [sb(f"part{j}", [P, 2, HALF], BF16) for j in range(NPART)]
        qs = [sb(f"qs{g}", [P, GH, S], BF16) for g in range(NG)]
        ks = [sb(f"ks{g}", [P, GH, S], BF16) for g in range(NG)]
        v = [sb(f"v{g}", [P, QT, GH, 2 * HD]) for g in range(NG)]
        mx = sb("mx", [P, 2, GH, QT])
        m_rest = sb("m_rest", [P, GH, QT])
        m_parts = sb("m_parts", [P, NPART, GH, QT], BF16)
        m_rows = sb("m_rows", [NPART * GH * QT, P], BF16)
        probs = sb("probs", [P, 2, GH, HALF])
        o_sum = sb("o_sum", [P, 2, HALF])
        o_turned = sb("o_turned", [P, 2, HALF])
        o_inv = sb("o_inv", [P, 2, HALF // 32, 1])
        o_norm = sb("o_norm", [P, 2, HALF])
        oT = sb("oT", [P, DC, S])
        x_d = sb("x_d", [P, 4, 2, D])
        y_d = sb("y_d", [P, 4, 2, D])
        gate = sb("gate", [P, 2, 2, D])
        s_d = sb("s_d", [P, 2, 2, D])
        g_d = sb("g_d", [P, 2, 2, D])
        out_d = sb("out_d", [P, 2, 2, D])

        ps_s = psum("ps_s", [P, GH, HALF])
        ps_m = psum("ps_m", [P, 2, HALF])
        ps_o = psum("ps_o", [P, HALF])
        ps_x = psum("ps_x", [P, HALF])

        consts_in, made, cleared = sem("consts_in"), sem("made"), sem("cleared")
        waited = sem("waited")
        xT_in = sem("xT_in")
        qk_ps, qk_done, rot_done = sem("qk_ps"), sem("qk_done"), sem("rot_done")
        qc_done, rs_done, roped, high_done = sem("qc_done"), sem("rs_done"), sem("roped"), sem("high_done")
        rest_done, mid_done, low_done = sem("rest_done"), sem("mid_done"), sem("low_done")
        stacked = [sem(f"stacked{g}") for g in range(NG)]
        pool_stacked = [sem(f"pool_stacked{g}") for g in range(NG)]
        v_ps, v_done = sem("v_ps"), sem("v_done")
        mx_ps, mx_done, mx_all = sem("mx_ps"), sem("mx_done"), sem("mx_all")
        m1, m2, m3, m_split = sem("m1"), sem("m2"), sem("m3"), sem("m_split")
        mt_ps, m_rows_done = sem("mt_ps"), sem("m_rows_done")
        m_in = [sem(f"m_in{g}") for g in range(NG)]
        s_ps, p_done, pv_done = sem("s_ps"), sem("p_done"), sem("pv_done")
        o_done, turned_done, inv_done = sem("o_done"), sem("turned_done"), sem("inv_done")
        scaled_done, norm_done = sem("scaled_done"), sem("norm_done")
        o_in = [sem("o_in0"), sem("o_in1")]
        xd_in = [sem(f"xd_in{j}") for j in range(4)]
        pr_ps, pr_done, gate_done = sem("pr_ps"), sem("pr_done"), sem("gate_done")
        gated, out_done = sem("gated"), sem("out_done")
        out_sent = [sem("out_sent0"), sem("out_sent1")]

        ROTATE = [(r + HD // 2) % HD + r // HD * HD for r in range(32)]
        first_units = [UNITS.index((half, 0)) for half in range(2)]
        NSTACK = 16 * 2 * GH * (len(TERMS_Q) - len(POOL_TERMS))
        NSTACK_POOL = 16 * 2 * GH * len(POOL_TERMS)
        D_UNIT = {5: 0, 6: 1, 7: 2, 8: 3}

        def width(u):
            half, kt = UNITS[u]
            return min(HALF, S - kt * P) if half else HALF - kt * P

        def diagonal(u):
            half, kt = UNITS[u]
            return kt // 4 == half

        def unit_chunks(u):
            return range(sum(UNIT_CHUNKS[:u]), sum(UNIT_CHUNKS[:u + 1]))

        def per_batch(engine, body):
            body(0, True, False)
            with engine.Fori(1, B - 1) as b:
                body(b, False, False)
            body(B - 1, False, True)

        def target(b, g, ahead):
            t = g + ahead
            return b + t // NG, t % NG, b * NG + t

        with nc.Block() as block:
            @block.sync
            def _(sp):
                sp.dma_start(const_f[:, 0, :], consts[:, 0:P]).then_inc(consts_in, 16)
                sp.dma_start(const_f[:, 1:3, :].rearrange("p a b -> p (a b)"), rope[:, 2 * S:2 * S + 2 * P]).then_inc(consts_in, 16)
                sp.dma_start(cos[:, :], rope[:, 0:S]).then_inc(consts_in, 16)
                sp.dma_start(sin[:, :], rope[:, S:2 * S]).then_inc(consts_in, 16)
                wq = w_qkv.rearrange("(c p) n -> p c n", p=P)
                for k in range(2):
                    for c in range(DC):
                        sp.dma_start(w_qk[:, c, :, k * GD:(k + 1) * GD],
                                     wq[:, c, k * D:(k + 1) * D].rearrange("p (g d) -> p g d", g=NG)).then_inc(consts_in, 16)
                sp.dma_start(w_v[:, :, :], wq[:, :, 2 * D:3 * D]).then_inc(consts_in, 16)
                sp.dma_start(w_o[:, :, :], w_proj.rearrange("(c p) n -> p c n", p=P)).then_inc(consts_in, 16)
                sp.dma_start(bias[:, 0, :], b_proj.partition_broadcast(P)).then_inc(consts_in, 16)

                def load_xT(b):
                    sp.dma_start(xT[:, 0], xnT_dram[b * 2]).then_inc(xT_in, 16)
                    sp.dma_start(xT[:, 1], xnT_dram[b * 2 + 1]).then_inc(xT_in, 16)

                def stack(g, q):
                    if not isinstance(q, int) or q >= NG:
                        sp.wait_ge(s_ps, (q - (NG - 1)) * NU * GH)
                    sp.wait_ge(low_done, q * 2 + 2)
                    for h in range(GH):
                        for t in range(len(TERMS_Q)):
                            if t not in POOL_TERMS:
                                r = slice(t * HD, (t + 1) * HD)
                                sp.dma_start(qs[g][r, h, :], parts[TERMS_Q[t]][h * HD:(h + 1) * HD]
                                             .rearrange("p a n -> p (a n)")).then_inc(stacked[g], 16)
                                sp.dma_start(ks[g][r, h, :], parts[TERMS_K[t]][GD + h * HD:GD + (h + 1) * HD]
                                             .rearrange("p a n -> p (a n)")).then_inc(stacked[g], 16)

                def send(b, j):
                    sp.wait_ge(out_done, b * 4 + (j + 1))
                    sp.dma_start(out[bass.ds(b * S + j * 2 * P, 2 * P)].rearrange("(t p) d -> p t d", p=P),
                                   out_d[:, j % 2]).then_inc(out_sent[j % 2], 16)

                load_xT(0)
                for q in range(AHEAD):
                    stack(q, q)

                def body(b, first, last):
                    for g in range(NG):
                        q = b * NG + g
                        if g == 0 and not last:
                            sp.wait_ge(v_ps, q + NG)
                            load_xT(b + 1)
                        if g == 3:
                            if not first:
                                sp.wait_ge(out_done, b * 4)
                            for j in range(4):
                                tok = bass.ds(b * S + j * 2 * P, 2 * P)
                                sp.dma_start(x_d[:, j], x[tok].rearrange("(t p) d -> p t d", p=P)).then_inc(xd_in[j], 16)
                                sp.dma_start(y_d[:, j], y_dram[tok].rearrange("(t p) d -> p t d", p=P)).then_inc(xd_in[j], 16)
                        if g == 0 and not first:
                            for j in range(4):
                                send(b - 1, j)
                        if not (last and g >= NG - AHEAD):
                            tb, tg, tq = target(b, g, AHEAD)
                            stack(tg, tq)
                per_batch(sp, body)
                for j in range(4):
                    send(B - 1, j)
                for j in range(2):
                    sp.wait_ge(out_sent[j], 16 * 2 * B)

            @block.gpsimd
            def _(pool):
                for g in range(NG):
                    if g > 0:
                        pool.wait_ge(cleared, 2 * g)
                    pool.memset(v[g][:, :, :, HD:2 * HD], 1.0).then_inc(cleared, 1)
                    pool.wait_ge(cleared, 2 * g + 1)
                    pool.memset(ks[g][NT:NT + 32], 1.0).then_inc(cleared, 1)
                pool.wait_ge(cleared, 2 * NG)
                pool.wait_ge(consts_in, 16 * 11)

                def rope_split(g, q):
                    a = q * 2
                    for n in range(2):
                        pool.wait_ge(qk_done, a + (n + 1))
                        if not isinstance(q, int) or q >= 1:
                            pool.wait_ge(low_done, a + (n - 1))
                        pool.sem_inc(waited, 1)
                        pool.tensor_tensor(qc[:, n], qk[:, n], cos[:, n * HALF:(n + 1) * HALF], ALU.mult).then_inc(qc_done, 1)
                        pool.wait_ge(rot_done, a + (n + 1))
                        pool.sem_inc(waited, 1)
                        pool.tensor_tensor(rs[:, n], rot[:, n], sin[:, n * HALF:(n + 1) * HALF], ALU.mult).then_inc(rs_done, 1)
                        pool.wait_ge(qc_done, a + (n + 1))
                        pool.wait_ge(rs_done, a + (n + 1))
                        pool.sem_inc(waited, 1)
                        pool.tensor_tensor(qc[:, n], qc[:, n], rs[:, n], ALU.add).then_inc(roped, 1)
                    for n in range(2):
                        pool.wait_ge(high_done, a + (n + 1))
                        pool.wait_ge(roped, a + (n + 1))
                        pool.sem_inc(waited, 1)
                        pool.tensor_tensor(rs[:, n], qc[:, n], parts[0][:, n], ALU.subtract).then_inc(rest_done, 1)
                    for n in range(2):
                        pool.wait_ge(mid_done, a + (n + 1))
                        pool.wait_ge(rest_done, a + (n + 1))
                        pool.sem_inc(waited, 1)
                        pool.tensor_tensor(parts[2][:, n], rs[:, n], parts[1][:, n], ALU.subtract).then_inc(low_done, 1)
                    if not isinstance(q, int) or q >= NG:
                        pool.wait_ge(s_ps, (q - (NG - 1)) * NU * GH)
                    pool.wait_ge(low_done, a + 2)
                    pool.sem_inc(waited, 1)
                    for h in range(GH):
                        for t in POOL_TERMS:
                            r = slice(t * HD, (t + 1) * HD)
                            pool.dma_start(qs[g][r, h, :], parts[TERMS_Q[t]][h * HD:(h + 1) * HD]
                                           .rearrange("p a n -> p (a n)")).then_inc(pool_stacked[g], 16)
                            pool.dma_start(ks[g][r, h, :], parts[TERMS_K[t]][GD + h * HD:GD + (h + 1) * HD]
                                           .rearrange("p a n -> p (a n)")).then_inc(pool_stacked[g], 16)

                def move_heads(g, q, half):
                    pool.wait_ge(norm_done, q * 2 + (half + 1))
                    pool.sem_inc(waited, 1)
                    for h in range(GH):
                        r = (g % 2) * GD + h * HD
                        pool.dma_start(oT[r:r + HD, g // 2, half * HALF:(half + 1) * HALF],
                                       o_norm[32 * h:32 * h + HD, half]).then_inc(o_in[half], 16)

                for q in range(AHEAD):
                    rope_split(q, q)

                def body(b, first, last):
                    for g in range(NG):
                        q = b * NG + g
                        if not (first and g == 0):
                            move_heads((g - 1) % NG, q - 1, 1)
                        if not (last and g >= NG - AHEAD):
                            tb, tg, tq = target(b, g, AHEAD)
                            rope_split(tg, tq)
                        if g == 0 and not first:
                            pool.wait_ge(pr_ps, b * 4)
                        move_heads(g, q, 0)
                per_batch(pool, body)
                move_heads(NG - 1, B * NG - 1, 1)

            @block.scalar
            def _(act):
                act.wait_ge(consts_in, 16 * 11)

                def qk_out(q, n):
                    if not isinstance(q, int) or q >= 1:
                        act.wait_ge(qc_done, q * 2 + (n - 1))
                        act.wait_ge(rot_done, q * 2 + (n - 1))
                    act.wait_ge(qk_ps, q * 2 + (n + 1))
                    act.activation(qk[:, n], ps_x[:, :], ACT.Copy).then_inc(qk_done, 1)

                def v_out(g, q):
                    if not isinstance(q, int) or q >= NG:
                        act.wait_ge(pv_done, (q - (NG - 1)) * NU)
                    act.wait_ge(v_ps, q + 1)
                    act.activation(v[g][:, :, :, 0:HD], ps_x[:, :].rearrange("p (t h d) -> p t h d", t=QT, h=GH),
                                   ACT.Copy).then_inc(v_done, 1)

                def high(g, q, n, stacked_before):
                    if n == 0 and stacked_before is not None:
                        act.wait_ge(stacked[(g - 1) % NG], stacked_before * NSTACK)
                        act.wait_ge(pool_stacked[(g - 1) % NG], stacked_before * NSTACK_POOL)
                    act.wait_ge(roped, q * 2 + (n + 1))
                    act.activation(parts[0][:, n], qc[:, n], ACT.Copy).then_inc(high_done, 1)

                def mid(q, n):
                    act.wait_ge(rest_done, q * 2 + (n + 1))
                    act.activation(parts[1][:, n], rs[:, n], ACT.Copy).then_inc(mid_done, 1)

                def max_rows(g, q):
                    if not isinstance(q, int) or q >= 1:
                        pg = (g - 1) % NG
                        act.wait_ge(m_in[pg], (q + (NG - 1 - pg)) // NG * 48 if isinstance(q, int) else
                                    (q - g) * 12 + (48 if g >= 1 else 0))
                    act.wait_ge(mt_ps, q + 1)
                    act.activation(m_rows[:, :], ps_x[0:NPART * GH * QT, 0:P // 2].bitcast(BF16), ACT.Copy).then_inc(m_rows_done, 1)
                    act.wait_ge(m_rows_done, q + 1)
                    for j in range(NPART):
                        act.dma_start(qs[g][NT + j:NT + j + 1].rearrange("o h (t n) -> o (h t) n", n=P),
                                      m_rows[j * GH * QT:(j + 1) * GH * QT]).then_inc(m_in[g], 16)

                def heads_out(q, half):
                    if not isinstance(q, int) or q >= 1:
                        act.wait_ge(norm_done, q * 2 + (half - 1))
                    act.wait_ge(pv_done, q * NU + (4 if half == 0 else NU))
                    act.activation(o_sum[:, half], ps_o[:, :], ACT.Copy).then_inc(o_done, 1)

                def gate_out(b, j):
                    if j >= 2:
                        act.wait_ge(gated, b * 4 + (j - 1))
                    act.wait_ge(xd_in[j], (b + 1) * 32)
                    act.activation(gate[:, j % 2], y_d[:, j], ACT.Silu).then_inc(gate_done, 1)

                for q in range(AHEAD):
                    qk_out(q, 0)
                    qk_out(q, 1)
                    v_out(q, q)
                    high(q, q, 0, 1 if q else None)
                    high(q, q, 1, None)
                    mid(q, 0)
                    mid(q, 1)
                max_rows(0, 0)

                def body(b, first, last):
                    for g in range(NG):
                        q = b * NG + g
                        project = not (last and g >= NG - AHEAD)
                        tb, tg, tq = target(b, g, AHEAD)
                        for u in range(NU):
                            if u == TURN_UNIT and not (last and g == NG - 1):
                                mb, mg, mq = target(b, g, 1)
                                max_rows(mg, mq)
                            for h in range(GH):
                                if h == 0 and not (first and g == 0 and u < 2):
                                    act.wait_ge(pv_done, q * NU + (u - 1))
                                act.wait_ge(s_ps, q * NU * GH + (u * GH + h + 1))
                                w = width(u)
                                act.activation(probs[:, u % 2, h, 0:w], ps_s[:, h, 0:w], ACT.Exp,
                                               scale=HD ** -0.5).then_inc(p_done, 1)
                            if u == 0 and not (first and g == 0):
                                heads_out(q - 1, 1)
                            if u == 4:
                                heads_out(q, 0)
                            if project:
                                if u == 0:
                                    qk_out(tq, 0)
                                if u == 2:
                                    qk_out(tq, 1)
                                if u == 4:
                                    v_out(tg, tq)
                                if u == 5:
                                    pb, pg, _ = target(b, g, AHEAD - 1)
                                    high(tg, tq, 0, pb + 1)
                                if u == 6:
                                    high(tg, tq, 1, None)
                                if u == 8:
                                    mid(tq, 0)
                                if u == 9:
                                    mid(tq, 1)
                            if u in D_UNIT and g == 0 and not first:
                                gate_out(b - 1, D_UNIT[u])
                per_batch(act, body)
                heads_out(B * NG - 1, 1)
                for j in range(4):
                    gate_out(B - 1, j)

            @block.vector
            def _(dve):
                dve.wait_ge(consts_in, 16 * 11)
                for j, dst in enumerate((ident, mask_qk, mask_kq)):
                    dve.tensor_copy(dst[:, :], const_f[:, j, :]).then_inc(made, 1)

                def turn(q, n):
                    if not isinstance(q, int) or q >= 1:
                        dve.wait_ge(rs_done, q * 2 + (n - 1))
                    dve.wait_ge(qk_done, q * 2 + (n + 1))
                    dve.sem_inc(waited, 1)
                    dve.stream_shuffle(rot[:, n], qk[:, n], ROTATE).then_inc(rot_done, 1)

                def reduce(q, c):
                    h, (qt, kh) = c // len(CHUNKS), CHUNKS[c % len(CHUNKS)]
                    w = min(HALF, (qt + 1) * P - kh * HALF)
                    if c == 0 and (not isinstance(q, int) or q >= 1):
                        dve.wait_ge(m_split, q)
                    dve.wait_ge(mx_ps, q * NCH + (c + 1))
                    dve.tensor_reduce(mx[:, kh, h, qt:qt + 1], ps_m[:, c % 2, 0:w], AX_X, ALU.max).then_inc(mx_done, 1)

                def split_max(q):
                    dve.wait_ge(mx_done, (q + 1) * NCH)
                    dve.tensor_tensor(mx[:, 0, :, 4:QT], mx[:, 0, :, 4:QT], mx[:, 1, :, 4:QT], ALU.max).then_inc(mx_all, 1)
                    if not isinstance(q, int) or q >= 1:
                        dve.wait_ge(mt_ps, q)
                    dve.wait_ge(mx_all, q + 1)
                    dve.tensor_scalar(m_parts[:, 0], mx[:, 0], -1.0, None, ALU.mult).then_inc(m1, 1)
                    dve.wait_ge(m1, q + 1)
                    dve.scalar_tensor_tensor(out=m_rest[:, :, :], in0=mx[:, 0], scalar=-1.0, in1=m_parts[:, 0],
                                             op0=ALU.mult, op1=ALU.subtract).then_inc(m2, 1)
                    dve.wait_ge(m2, q + 1)
                    dve.tensor_copy(m_parts[:, 1], m_rest[:, :, :]).then_inc(m3, 1)
                    dve.wait_ge(m3, q + 1)
                    dve.tensor_tensor(m_parts[:, 2], m_rest[:, :, :], m_parts[:, 1], ALU.subtract).then_inc(m_split, 1)

                def normalise(b, g, q, half):
                    k = q * 2 + half
                    dve.wait_ge(o_done, k + 1)
                    dve.transpose(o_turned[:, half], o_sum[:, half]).then_inc(turned_done, 1)
                    blocks = o_turned[:, half].rearrange("p (t d) -> p t d", d=32)
                    dve.wait_ge(turned_done, k + 1)
                    dve.reciprocal(o_inv[:, half], blocks[:, :, HD:HD + 1]).then_inc(inv_done, 1)
                    dve.wait_ge(inv_done, k + 1)
                    dve.tensor_tensor(blocks[:, :, 0:HD], blocks[:, :, 0:HD],
                                      o_inv[:, half].to_broadcast([P, HALF // 32, HD]), ALU.mult).then_inc(scaled_done, 1)
                    if not isinstance(q, int) or q >= 1:
                        dve.wait_ge(o_in[half], q * 64)
                    dve.wait_ge(scaled_done, k + 1)
                    dve.transpose(o_norm[:, half], o_turned[:, half]).then_inc(norm_done, 1)

                def finish(b, j):
                    k = b * 4 + j
                    dve.wait_ge(pr_ps, k + 1)
                    dve.tensor_tensor(s_d[:, j % 2], ps_x[:, :].rearrange("p (t d) -> p t d", t=2),
                                      bias[:, :, :].to_broadcast([P, 2, D]), ALU.add).then_inc(pr_done, 1)
                    if j >= 2:
                        dve.wait_ge(out_done, b * 4 + (j - 1))
                    dve.wait_ge(gate_done, k + 1)
                    dve.wait_ge(pr_done, k + 1)
                    dve.tensor_tensor(g_d[:, j % 2], s_d[:, j % 2], gate[:, j % 2], ALU.mult).then_inc(gated, 1)
                    if j >= 2:
                        dve.wait_ge(out_sent[j % 2], b * 32 + 16)
                    dve.wait_ge(gated, k + 1)
                    dve.tensor_tensor(out_d[:, j % 2], g_d[:, j % 2], x_d[:, j], ALU.add).then_inc(out_done, 1)

                for q in range(AHEAD):
                    turn(q, 0)
                    turn(q, 1)
                for c in range(NCH):
                    reduce(0, c)
                split_max(0)

                def body(b, first, last):
                    for g in range(NG):
                        q = b * NG + g
                        if g == NG - 1 and not first:
                            dve.wait_ge(out_sent[0], b * 32)
                            dve.wait_ge(out_sent[1], b * 32)
                        for u in range(NU):
                            if not (last and g == NG - 1):
                                for c in unit_chunks(u):
                                    reduce(q + 1, c)
                                if u == len(UNIT_CHUNKS) - 1:
                                    split_max(q + 1)
                            if u == 0 and not (last and g >= NG - AHEAD):
                                turn(target(b, g, AHEAD)[2], 0)
                            if u == 2 and not (last and g >= NG - AHEAD):
                                turn(target(b, g, AHEAD)[2], 1)
                            if u == 1 and not (first and g == 0):
                                normalise(b, (g - 1) % NG, q - 1, 1)
                            if u == 5:
                                normalise(b, g, q, 0)
                            if u in D_UNIT and g == 0 and not first:
                                finish(b - 1, D_UNIT[u])
                per_batch(dve, body)
                normalise(B, NG - 1, B * NG - 1, 1)
                for j in range(4):
                    finish(B - 1, j)

            @block.tensor
            def _(pe):
                pe.wait_ge(made, 3)
                pe.wait_ge(cleared, 2 * NG)
                pe.wait_ge(consts_in, 16 * 11)

                def project_qk(g, q, n, xT_count):
                    if n == 0:
                        if xT_count is not None:
                            pe.wait_ge(xT_in, xT_count)
                        if not isinstance(q, int) or q >= AHEAD:
                            pe.wait_ge(m_rows_done, q - AHEAD + 1)
                        elif q > 0:
                            pe.wait_ge(v_done, q)
                    else:
                        pe.wait_ge(qk_done, q * 2 + 1)
                    for c in range(DC):
                        last = pe.matmul(ps_x[:, :], w_qk[:, c, g, :], xT[:, n, c, :], start=(c == 0), stop=(c == DC - 1))
                        if c == DC - 1:
                            last.then_inc(qk_ps, 1)
                        yield

                def project_v(g, q):
                    pe.wait_ge(qk_done, q * 2 + 2)
                    for t in range(QT):
                        for c in range(DC):
                            last = pe.matmul(ps_x[:, t * GD:(t + 1) * GD], xT[:, t // 4, c, (t % 4) * P:(t % 4 + 1) * P],
                                             w_v[:, c, g * GD:(g + 1) * GD], start=(c == 0), stop=(c == DC - 1))
                        if t == QT - 1:
                            last.then_inc(v_ps, 1)
                        if t % 2:
                            yield

                def max_scores(g, q, c):
                    h, (qt, kh) = c // len(CHUNKS), CHUNKS[c % len(CHUNKS)]
                    w = min(HALF, (qt + 1) * P - kh * HALF)
                    diag = kh == qt // 4
                    if not (isinstance(q, int) and q == 0 and c < 2):
                        pe.wait_ge(mx_done, q * NCH + (c - 1))
                    last = pe.matmul(ps_m[:, c % 2, 0:w], qs[g][0:NT, h, qt * P:(qt + 1) * P],
                                     ks[g][0:NT, h, kh * HALF:kh * HALF + w], start=True, stop=not diag)
                    if diag:
                        last = pe.matmul(ps_m[:, c % 2, w - P:w], ident[:, :], mask_qk[:, :], start=False, stop=True)
                    last.then_inc(mx_ps, 1)

                def turn_max(q, before):
                    before()
                    pe.wait_ge(m_split, q + 1)
                    pe.transpose(ps_x[0:NPART * GH * QT, 0:P // 2].bitcast(BF16),
                                 m_parts[:, :, :, :].rearrange("p a h t -> p (a h t)"), ident[:, :]).then_inc(mt_ps, 1)

                def scores(g, q, u, h, free):
                    half, kt = UNITS[u]
                    w = width(u)
                    q0 = half * HALF + HALF - w
                    if free is not None:
                        pe.wait_ge(p_done, free)
                    last = pe.matmul(ps_s[:, h, 0:w], ks[g][0:NT + NPART, h, kt * P:(kt + 1) * P],
                                     qs[g][0:NT + NPART, h, q0:q0 + w], start=True, stop=not diagonal(u))
                    if diagonal(u):
                        last = pe.matmul(ps_s[:, h, 0:P], ident[:, :], mask_kq[:, :], start=False, stop=True)
                    last.then_inc(s_ps, 1)

                def values(g, q, u):
                    half, kt = UNITS[u]
                    w = width(u)
                    if u in first_units and not (isinstance(q, int) and q * 2 + half == 0):
                        pe.wait_ge(o_done, q * 2 + half)
                    pe.wait_ge(p_done, q * NU * GH + (u + 1) * GH)
                    for h in range(GH):
                        last = pe.matmul(ps_o[32 * h:32 * h + 32, HALF - w:HALF], v[g][:, kt, h, :], probs[:, u % 2, h, 0:w],
                                         start=u in first_units, stop=u + 1 in (first_units[1], NU), skip_group_check=True)
                    last.then_inc(pv_done, 1)

                def project_out(b, j, first_of_batch):
                    if j == 0:
                        pe.wait_ge(o_in[0], (b + 1) * 256)
                        pe.wait_ge(o_in[1], (b + 1) * 256)
                        first_of_batch()
                    else:
                        pe.wait_ge(pr_done, b * 4 + j)
                    for t in range(2):
                        for c in range(DC):
                            col = (2 * j + t) * P
                            last = pe.matmul(ps_x[:, t * D:(t + 1) * D], oT[:, c, col:col + P], w_o[:, c, :],
                                             start=(c == 0), stop=(c == DC - 1))
                    last.then_inc(pr_ps, 1)

                for q in range(AHEAD):
                    for part in (project_qk(q, q, 0, 32 if q == 0 else None), project_qk(q, q, 1, None), project_v(q, q)):
                        for _ in part:
                            pass
                pe.wait_ge(stacked[0], NSTACK)
                pe.wait_ge(pool_stacked[0], NSTACK_POOL)
                for c in range(NCH):
                    max_scores(0, 0, c)
                turn_max(0, lambda: pe.wait_ge(v_done, AHEAD))

                def body(b, first, last):
                    for g in range(NG):
                        q = b * NG + g
                        project = not (last and g >= NG - AHEAD)
                        tb, tg, tq = target(b, g, AHEAD)
                        nb, ng, nq = target(b, g, 1)
                        find_max = not (last and g == NG - 1)
                        for u in range(NU):
                            if u == 0:
                                pe.wait_ge(m_in[g], (b + 1) * 48)
                                if find_max:
                                    pe.wait_ge(stacked[ng], (nb + 1) * NSTACK)
                                    pe.wait_ge(pool_stacked[ng], (nb + 1) * NSTACK_POOL)
                            if u == TURN_UNIT and find_max:
                                def before():
                                    if g == 0 and not first:
                                        pe.wait_ge(pr_done, b * 4)
                                    elif project:
                                        pe.wait_ge(v_done, tq + 1)
                                    else:
                                        pe.wait_ge(m_rows_done, q + 1)
                                turn_max(nq, before)

                            def pieces():
                                for h in range(GH):
                                    free = None if (first and g == 0 and u == 0) else q * NU * GH + ((u - 1) * GH + h + 1)
                                    scores(g, q, u, h, free)
                                    yield
                                if project and u == 0:
                                    yield from project_qk(tg, tq, 0, (tb + 1) * 32 if tg == 0 else None)
                                if project and u == 2:
                                    yield from project_qk(tg, tq, 1, None)
                                if project and u == 4:
                                    yield from project_v(tg, tq)
                                if u in D_UNIT and g == 0 and not first:
                                    project_out(b - 1, D_UNIT[u], lambda: pe.wait_ge(v_done, tq + 1))
                                    yield
                                if u > 0:
                                    values(g, q, u - 1)
                                elif not (first and g == 0):
                                    values((g - 1) % NG, q - 1, NU - 1)
                                yield

                            chunks = list(unit_chunks(u)) if find_max else []
                            count = 4 + 1 + (project and u in (0, 2)) * DC + (project and u == 4) * QT // 2 + (
                                u in D_UNIT and g == 0 and not first)
                            for n, _ in enumerate(pieces()):
                                while chunks and (len(unit_chunks(u)) - len(chunks)) * count < (n + 1) * len(unit_chunks(u)):
                                    max_scores(ng, nq, chunks.pop(0))
                per_batch(pe, body)
                values(NG - 1, B * NG - 1, NU - 1)
                for j in range(4):
                    project_out(B - 1, j, lambda: pe.wait_ge(m_rows_done, B * NG))


def build(nc, x, w_qkv, w_proj, b_proj, gate_w, shared_gate_w, shared_gu_w, shared_down_w, expert_gu_w, expert_down_w,
          consts, rope, out):
    xnT_dram = nc.dram_tensor("xnT_dram", [NBLK, P, DC, BLK], F32).ap()
    cum_dram = nc.dram_tensor("cum_dram", [E, TOK], F32).ap()
    wts_dram = nc.dram_tensor("wts_dram", [TOK, E], F32).ap()
    ends_dram = nc.dram_tensor("ends_dram", [E, NTILE], F32).ap()
    y_dram = nc.dram_tensor("y_dram", [TOK, D], F32).ap()
    feed_forward(nc, x, gate_w, shared_gate_w, shared_gu_w, shared_down_w, expert_gu_w, expert_down_w,
                 consts, xnT_dram, y_dram, cum_dram, wts_dram, ends_dram)
    experts(nc, x, expert_gu_w, expert_down_w, consts, y_dram, cum_dram, wts_dram, ends_dram)
    attention(nc, x, w_qkv, w_proj, b_proj, consts, rope, xnT_dram, y_dram, out)


def constants():
    c = np.zeros((P, 3 * P + 2 * E), np.float32)
    c[:, 0:P] = np.eye(P)
    c[:, P:2 * P] = np.triu(np.ones((P, P)))
    c[:, 2 * P] = np.arange(P)
    c[:, 3 * P:3 * P + E] = P * np.arange(E)
    c[:, 3 * P + E:] = np.arange(E)
    return c


def rope_tables():
    inv_freq = (1.0 / 10000.0 ** (np.arange(0, HD, 2, dtype=np.float32) / np.float32(HD))).astype(np.float32)
    angle = (np.arange(S, dtype=np.float32)[:, None] * inv_freq[None, :]).astype(np.float32)
    cos, sin = np.cos(angle).T, np.sin(angle).T
    r = np.zeros((P, 2 * S + 2 * P), np.float32)
    r[:, 0:S] = np.tile(np.concatenate([cos, cos]), (P // HD, 1))
    r[:, S:2 * S] = np.tile(np.concatenate([-sin, sin]), (P // HD, 1))
    later = np.triu(np.ones((P, P), np.float32), 1) * MASKED
    r[:, 2 * S:2 * S + P] = later
    r[:, 2 * S + P:] = later.T
    return r


_INS = ['L0_attn_x', 'L0_attn_w_qkv', 'L0_attn_w_proj', 'L0_attn_b_proj', 'L0_ffn_gate_w', 'L0_ffn_shared_gate_w',
        'L0_ffn_shared_gate_up_w', 'L0_ffn_shared_down_w', 'L0_ffn_expert_gate_up_w', 'L0_ffn_expert_down_w']


def kernel(**inputs):
    import numpy as _np
    import concourse.bacc as _bacc
    from concourse import mybir as _mybir
    from concourse.bass_utils import run_bass_kernel_spmd as _run

    nc = _bacc.Bacc("TRN2", target_bir_lowering=False, num_devices=1)
    arrays, args = {}, []
    layouts = {name: _np.asarray(inputs[name]) for name in _INS}
    layouts['L0_attn_x'] = layouts['L0_attn_x'].reshape(TOK, D)
    layouts['constants'] = constants()
    layouts['rope'] = rope_tables()
    for name, a in layouts.items():
        a = _np.ascontiguousarray(a)
        arrays[f"in_{name}_dram"] = a
        args.append(nc.dram_tensor(f"in_{name}_dram", a.shape, _mybir.dt.from_np(a.dtype), kind="ExternalInput").ap())
    args.append(nc.dram_tensor("out_0_dram", (TOK, D), _mybir.dt.float32, kind="ExternalOutput").ap())
    build(nc, *args)
    r = _run(nc, [arrays], core_ids=[0])
    return r.results[0]["out_0_dram"].reshape(B, S, D)
```

```python
from contextlib import ExitStack

import concourse.bass as bass
import numpy as np
from concourse import mybir

F32 = mybir.dt.float32
BF16 = mybir.dt.bfloat16
I32 = mybir.dt.int32
ACT = mybir.ActivationFunctionType
ALU = mybir.AluOpType
AX_X = mybir.AxisListType.X

P = 128
B, S, D = 16, 1024, 256
TOK = B * S
E, CAP, TOPK = 64, 128, 8
IS, IE = 512, 128
DC = D // P
BLK = 512
BT = BLK // P
NBLK = TOK // BLK
NTILE = TOK // P
EPS = 1e-5
MASKED = -1e30
LOWEST = -3e38


def feed_forward(nc, x, gate_w, shared_gate_w, shared_gu_w, shared_down_w, expert_gu_w, expert_down_w,
                 consts, xnT_dram, y_dram, cum_dram, table_dram, ends_dram):
    with ExitStack() as ctx:
        def sb(name, shape, dt=F32):
            return ctx.enter_context(nc.sbuf_tensor(name, shape, dt))

        def psum(name, shape):
            return ctx.enter_context(nc.psum_tensor(name, shape, F32))

        def sem(name):
            return ctx.enter_context(nc.semaphore(name))

        w_router = sb("w_router", [P, DC, E + 1])
        w_gu = sb("w_gu", [P, DC, 2 * IS])
        w_down = sb("w_down", [P, IS // P, D])
        ident = sb("ident", [P, P])
        tri_f = sb("tri_f", [P, P])
        tri = sb("tri", [P, P], BF16)
        ones = sb("ones", [P, P], BF16)
        neg_half = sb("neg_half", [P, BT])
        x_t = sb("x_t", [P, 2, BT, D])
        stats = sb("stats", [P, 2, BT, 6])
        meanvar = sb("meanvar", [P, 2, BT, 2])
        var_eps = sb("var_eps", [P, 2, BT])
        rstd = sb("rstd", [P, 2, BT])
        xn = sb("xn", [P, 2, BT, D])
        xnT = sb("xnT", [P, 2, DC, BLK])
        logits = sb("logits", [P, 2, BT, E + 1])
        top = sb("top", [P, 2, BT, TOPK])
        rest = sb("rest", [P, 2, BT, E])
        chosen = sb("chosen", [P, 2, BT, E], BF16)
        shifted = sb("shifted", [P, 2, BT, E])
        expo = sb("expo", [P, 2, BT, E])
        picked = sb("picked", [P, 2, BT, E])
        picked_sum = sb("picked_sum", [P, 2, BT])
        picked_inv = sb("picked_inv", [P, 2, BT])
        wts = sb("wts", [P, 2, BT, E])
        gate_exp = sb("gate_exp", [P, 2, BT])
        gate_den = sb("gate_den", [P, 2, BT])
        gate_sig = sb("gate_sig", [P, 2, BT])
        base = sb("base", [E, 1])
        cum = sb("cum", [E, 2, BLK])
        ends = sb("ends", [E, NTILE])
        silu = sb("silu", [P, 2, BLK])
        act = sb("act", [P, IS // P, BLK])
        y_t = sb("y_t", [P, 2, BT, D])

        ps_td = psum("ps_td", [P, 2, 512])
        ps_router = psum("ps_router", [P, BT, E + 1])
        ps_cum = psum("ps_cum", [E, BLK])
        ps_gu = psum("ps_gu", [P, 2, 2, 512])

        waited = sem("waited")
        weights_in = sem("weights_in")
        consts_in = sem("consts_in")
        setup = sem("setup")
        x_in = [sem("x_in0"), sem("x_in1")]
        stats_done = sem("stats_done")
        var_done = sem("var_done")
        rstd_done = sem("rstd_done")
        stats_step = sem("stats_step")
        xn_done = sem("xn_done")
        transposed = sem("transposed")
        xnT_done = sem("xnT_done")
        xn_out = [sem("xn_out0"), sem("xn_out1")]
        xnT_out = [sem("xnT_out0"), sem("xnT_out1")]
        router_done = sem("router_done")
        logits_done = sem("logits_done")
        top_done = sem("top_done")
        rest_done = sem("rest_done")
        chosen_done = sem("chosen_done")
        shifted_done = sem("shifted_done")
        expo_done = sem("expo_done")
        gate_exp_done = sem("gate_exp_done")
        picked_done = sem("picked_done")
        sum_done = sem("sum_done")
        inv_done = sem("inv_done")
        gate_den_done = sem("gate_den_done")
        wts_done = sem("wts_done")
        wts_out = [sem("wts_out0"), sem("wts_out1")]
        gate_done = sem("gate_done")
        counted = sem("counted")
        cum_done = sem("cum_done")
        base_done = sem("base_done")
        ends_done = sem("ends_done")
        cum_out = [sem("cum_out0"), sem("cum_out1")]
        gu_done = sem("gu_done")
        silu_done = sem("silu_done")
        act_done = sem("act_done")
        down_done = sem("down_done")
        y_done = sem("y_done")
        y_out = [sem("y_out0"), sem("y_out1")]
        ends_out = sem("ends_out")

        NJ = IS // P
        x_b = x.rearrange("(n t p) d -> n p t d", t=BT, p=P)
        y_b = y_dram.rearrange("(n t p) d -> n p t d", t=BT, p=P)
        table_b = table_dram.rearrange("(n t p) e -> n p t e", t=BT, p=P)

        def per_block(engine, step):
            for u in range(2):
                step(u, u, 0, True, False)
            with engine.Fori(1, NBLK // 2 - 1) as i:
                for u in range(2):
                    step(i * 2 + u, u, i, False, False)
            for u in range(2):
                step(NBLK - 2 + u, u, NBLK // 2 - 1, False, u == 1)

        def following(n, u, i):
            return n + 1, 1 - u, i + u, isinstance(n, int) and n < 1

        with nc.Block() as block:
            @block.sync
            def _(sp):
                sp.dma_start(ident[:, :], consts[:, 0:P]).then_inc(consts_in, 16)
                sp.dma_start(tri_f[:, :], consts[:, P:2 * P]).then_inc(consts_in, 16)
                sp.dma_start(w_router[:, :, 0:E], gate_w.rearrange("(c p) e -> p c e", p=P),
                             allow_slow_non_contiguous=True).then_inc(weights_in, 16)
                sp.dma_start(w_router[:, :, E:E + 1], shared_gate_w.rearrange("(c p) e -> p c e", p=P),
                             allow_slow_non_contiguous=True).then_inc(weights_in, 16)
                sp.dma_start(w_gu[:, :, :], shared_gu_w.rearrange("(c p) f -> p c f", p=P)).then_inc(weights_in, 16)
                sp.dma_start(w_down[:, :, :], shared_down_w.rearrange("(c p) f -> p c f", p=P)).then_inc(weights_in, 16)

                def store(n, u):
                    sp.wait_ge(xn_done, (n + 1) * BT)
                    sp.dma_start(table_b[n, :, :, 0:D], xn[:, u]).then_inc(xn_out[u], 16)

                def work(n, u, i, early, last):
                    if not early:
                        sp.wait_ge(xn_done, (n - 1) * BT)
                    sp.dma_start(x_t[:, u], x_b[n]).then_inc(x_in[u], 16)
                    if not (early and u == 0):
                        store(n - 1, 1 - u)
                per_block(sp, work)
                store(NBLK - 1, 1)
                for u in range(2):
                    sp.wait_ge(xn_out[u], 16 * (NBLK // 2))

            @block.gpsimd
            def _(pool):
                pool.memset(neg_half[:, :], -0.5).then_inc(setup, 1)
                pool.memset(ones[:, :], 1.0).then_inc(setup, 1)
                pool.wait_ge(setup, 2)

                def invert(n, u, i, early):
                    if not early:
                        pool.wait_ge(xn_done, (n - 1) * BT)
                    pool.wait_ge(var_done, n + 1)
                    pool.tensor_tensor(rstd[:, u], var_eps[:, u], neg_half[:, :], ALU.pow).then_inc(rstd_done, 1)

                def finish(n, u, i, early, last):
                    if not last:
                        invert(*following(n, u, i))
                    pool.wait_ge(wts_done, n + 1)
                    pool.sem_inc(waited, 1)
                    pool.dma_start(table_b[n, :, :, D:D + E], wts[:, u]).then_inc(wts_out[u], 16)
                    pool.wait_ge(cum_done, n + 1)
                    pool.sem_inc(waited, 1)
                    pool.dma_start(cum_dram[:, bass.ds(n * BLK, BLK)], cum[:, u]).then_inc(cum_out[u], 16)
                    pool.wait_ge(y_done, (n + 1) * BT)
                    pool.sem_inc(waited, 1)
                    pool.dma_start(y_b[n], y_t[:, u]).then_inc(y_out[u], 16)
                invert(0, 0, 0, True)
                per_block(pool, finish)
                pool.wait_ge(ends_done, NBLK)
                pool.dma_start(ends_dram, ends[:, :]).then_inc(ends_out, 16)
                pool.wait_ge(ends_out, 16)
                for u in range(2):
                    pool.wait_ge(wts_out[u], 16 * (NBLK // 2))
                    pool.wait_ge(cum_out[u], 16 * (NBLK // 2))
                    pool.wait_ge(y_out[u], 16 * (NBLK // 2))

            @block.scalar
            def _(act_e):
                def turned(n, u, i, early):
                    if not early:
                        act_e.wait_ge(xnT_out[u], i * 16)
                        act_e.wait_ge(gu_done, (n - 1) * NJ)
                        act_e.wait_ge(router_done, n - 1)
                    for c in range(DC):
                        act_e.wait_ge(transposed, n * DC + (c + 1))
                        act_e.activation(xnT[:, u, c, :], ps_td[:, c, :], ACT.Copy).then_inc(xnT_done, 1)
                    act_e.wait_ge(xnT_done, (n + 1) * DC)
                    act_e.dma_start(xnT_dram[n], xnT[:, u]).then_inc(xnT_out[u], 16)

                def work(n, u, i, early, last):
                    if not early:
                        act_e.wait_ge(picked_done, n - 1)
                        act_e.wait_ge(gate_den_done, n - 1)
                    act_e.wait_ge(shifted_done, n + 1)
                    act_e.activation(expo[:, u], shifted[:, u], ACT.Exp).then_inc(expo_done, 1)
                    act_e.activation(gate_exp[:, u], logits[:, u, :, E], ACT.Exp, scale=-1.0).then_inc(gate_exp_done, 1)
                    for j in range(NJ):
                        if not (early and u == 0 and j < 2):
                            act_e.wait_ge(act_done, n * NJ + (j - 1))
                        act_e.wait_ge(gu_done, n * NJ + (j + 1))
                        act_e.activation(silu[:, j % 2, :], ps_gu[:, j % 2, 0, :], ACT.Silu).then_inc(silu_done, 1)
                    if not last:
                        turned(*following(n, u, i))
                    if not early:
                        act_e.wait_ge(y_out[u], i * 16)
                    act_e.wait_ge(gate_done, n + 1)
                    for t in range(BT):
                        if t % 2 == 0:
                            act_e.wait_ge(down_done, n * BT + (t + 2))
                        act_e.activation(y_t[:, u, t, :], ps_td[:, t // 2, (t % 2) * D:(t % 2 + 1) * D], ACT.Copy,
                                         scale=gate_sig[:, u, t:t + 1]).then_inc(y_done, 1)
                turned(0, 0, 0, True)
                per_block(act_e, work)
                for u in range(2):
                    act_e.wait_ge(xnT_out[u], 16 * (NBLK // 2))

            @block.vector
            def _(dve):
                dve.wait_ge(consts_in, 32)
                dve.tensor_copy(tri[:, :], tri_f[:, :]).then_inc(setup, 1)
                dve.memset(base[:, :], 0.0).then_inc(base_done, 1)

                def moments(n, u, i, early):
                    dve.wait_ge(x_in[u], i * 16 + 16)
                    for t in range(BT):
                        if not early and t == 0:
                            dve.wait_ge(stats_step, (n - 1) * BT)
                        dve.bn_stats(stats[:, u, t, :], x_t[:, u, t, :]).then_inc(stats_done, 1)
                    if not early:
                        dve.wait_ge(xn_done, (n - 1) * BT)
                    for t in range(BT):
                        dve.wait_ge(stats_done, n * BT + (t + 1))
                        dve.sem_inc(waited, 1)
                        dve.bn_aggr(meanvar[:, u, t, :], stats[:, u, t, :]).then_inc(stats_step, 1)
                    dve.wait_ge(stats_step, (n + 1) * BT)
                    dve.tensor_scalar(var_eps[:, u], meanvar[:, u, :, 1], EPS, None, ALU.add).then_inc(var_done, 1)

                def normalise(n, u, i, early):
                    if not early:
                        dve.wait_ge(transposed, (n - 1) * DC)
                        dve.wait_ge(xn_out[u], i * 16)
                    dve.wait_ge(rstd_done, n + 1)
                    for t in range(BT):
                        dve.tensor_scalar(xn[:, u, t, :], x_t[:, u, t, :], meanvar[:, u, t, 0:1],
                                          rstd[:, u, t:t + 1], ALU.subtract, ALU.mult).then_inc(xn_done, 1)

                def work(n, u, i, early, last):
                    if not early:
                        dve.wait_ge(gate_exp_done, n - 1)
                    dve.wait_ge(router_done, n + 1)
                    dve.tensor_copy(logits[:, u], ps_router[:, :, :]).then_inc(logits_done, 1)
                    dve.wait_ge(logits_done, n + 1)
                    dve.sem_inc(waited, 1)
                    for t in range(BT):
                        dve.max(top[:, u, t, :], logits[:, u, t, 0:E]).then_inc(top_done, 1)
                    for t in range(BT):
                        dve.wait_ge(top_done, n * BT + (t + 1))
                        dve.sem_inc(waited, 1)
                        dve.match_replace(rest[:, u, t, :], top[:, u, t, :], logits[:, u, t, 0:E], LOWEST).then_inc(rest_done, 1)
                    if not early:
                        dve.wait_ge(counted, n - 1)
                    dve.wait_ge(rest_done, (n + 1) * BT)
                    dve.tensor_tensor(chosen[:, u], rest[:, u], logits[:, u, :, 0:E], ALU.not_equal).then_inc(chosen_done, 1)
                    dve.tensor_tensor(shifted[:, u], logits[:, u, :, 0:E],
                                      top[:, u, :, 0:1].to_broadcast([P, BT, E]), ALU.subtract).then_inc(shifted_done, 1)

                    def gated(j):
                        if not (early and u == 0) and j == 0:
                            dve.wait_ge(down_done, n * BT)
                        dve.wait_ge(silu_done, n * NJ + (j + 1))
                        dve.tensor_tensor(act[:, j, :], silu[:, j % 2, :], ps_gu[:, j % 2, 1, :], ALU.mult).then_inc(act_done, 1)

                    gated(0)
                    dve.wait_ge(expo_done, n + 1)
                    dve.tensor_tensor(picked[:, u], expo[:, u], chosen[:, u], ALU.mult).then_inc(picked_done, 1)
                    dve.wait_ge(gate_exp_done, n + 1)
                    dve.tensor_scalar(gate_den[:, u], gate_exp[:, u], 1.0, None, ALU.add).then_inc(gate_den_done, 1)
                    dve.wait_ge(picked_done, n + 1)
                    dve.tensor_reduce(picked_sum[:, u], picked[:, u], AX_X, ALU.add).then_inc(sum_done, 1)
                    if not early:
                        dve.wait_ge(y_done, (n - 1) * BT)
                    dve.wait_ge(gate_den_done, n + 1)
                    dve.reciprocal(gate_sig[:, u], gate_den[:, u]).then_inc(gate_done, 1)
                    dve.wait_ge(sum_done, n + 1)
                    dve.reciprocal(picked_inv[:, u], picked_sum[:, u]).then_inc(inv_done, 1)
                    if not last:
                        moments(*following(n, u, i))
                    gated(1)
                    if not early:
                        dve.wait_ge(wts_out[u], i * 16)
                    dve.wait_ge(inv_done, n + 1)
                    dve.tensor_tensor(wts[:, u], picked[:, u],
                                      picked_inv[:, u].unsqueeze(2).to_broadcast([P, BT, E]), ALU.mult).then_inc(wts_done, 1)
                    if not last:
                        normalise(*following(n, u, i))
                    gated(2)
                    if not early:
                        dve.wait_ge(cum_out[u], i * 16)
                    dve.wait_ge(counted, n + 1)
                    dve.wait_ge(base_done, n + 1)
                    dve.tensor_scalar(cum[:, u], ps_cum[:, :], base[:, 0:1], None, ALU.add).then_inc(cum_done, 1)
                    gated(3)
                    dve.wait_ge(cum_done, n + 1)
                    dve.tensor_copy(base[:, :], cum[:, u, BLK - 1:BLK]).then_inc(base_done, 1)
                    dve.tensor_copy(ends[:, bass.ds(n * BT, BT)], cum[:, u, P - 1:BLK:P]).then_inc(ends_done, 1)
                moments(0, 0, 0, True)
                normalise(0, 0, 0, True)
                per_block(dve, work)

            @block.tensor
            def _(pe):
                pe.wait_ge(setup, 3)
                pe.wait_ge(consts_in, 32)
                pe.wait_ge(weights_in, 64)

                def turn(n, u, i, early):
                    if not early:
                        pe.wait_ge(y_done, (n - 1) * BT)
                    pe.wait_ge(xn_done, (n + 1) * BT)
                    for c in range(DC):
                        for t in range(BT):
                            last = pe.transpose(ps_td[:, c, t * P:(t + 1) * P], xn[:, u, t, c * P:(c + 1) * P], ident[:, :])
                        last.then_inc(transposed, 1)

                def work(n, u, i, early, last_block):
                    if not (early and u == 0):
                        pe.wait_ge(logits_done, n)
                    pe.wait_ge(xnT_done, (n + 1) * DC)
                    for t in range(BT):
                        for c in range(DC):
                            last = pe.matmul(ps_router[:, t, :], xnT[:, u, c, t * P:(t + 1) * P], w_router[:, c, :],
                                             start=(c == 0), stop=(c == DC - 1))
                    last.then_inc(router_done, 1)
                    for j in range(NJ):
                        if not (early and u == 0 and j < 2):
                            pe.wait_ge(act_done, n * NJ + (j - 1))
                        for k in range(2):
                            for c in range(DC):
                                f = k * IS + j * P
                                last = pe.matmul(ps_gu[:, j % 2, k, :], w_gu[:, c, f:f + P], xnT[:, u, c, :],
                                                 start=(c == 0), stop=(c == DC - 1))
                        last.then_inc(gu_done, 1)
                    if not last_block:
                        turn(*following(n, u, i))
                    if not (early and u == 0):
                        pe.wait_ge(cum_done, n)
                    pe.wait_ge(chosen_done, n + 1)
                    for t in range(BT):
                        for before in range(t):
                            pe.matmul(ps_cum[:, t * P:(t + 1) * P], chosen[:, u, before, :], ones[:, :],
                                      start=(before == 0), stop=False)
                        last = pe.matmul(ps_cum[:, t * P:(t + 1) * P], chosen[:, u, t, :], tri[:, :],
                                         start=(t == 0), stop=True)
                    last.then_inc(counted, 1)
                    if not last_block:
                        pe.wait_ge(xnT_done, (n + 2) * DC)
                    pe.wait_ge(act_done, (n + 1) * NJ)
                    for t in range(BT):
                        for j in range(NJ):
                            last = pe.matmul(ps_td[:, t // 2, (t % 2) * D:(t % 2 + 1) * D], act[:, j, t * P:(t + 1) * P],
                                             w_down[:, j, :], start=(j == 0), stop=(j == NJ - 1))
                        last.then_inc(down_done, 1)
                turn(0, 0, 0, True)
                per_block(pe, work)


NRING = 8
NCHK = E // NRING
FIRST = 2 * NRING
GATHERED = 5


def experts(nc, expert_gu_w, expert_down_w, consts, y_dram, cum_dram, table_dram, ends_dram):
    with ExitStack() as ctx:
        def sb(name, shape, dt=F32):
            return ctx.enter_context(nc.sbuf_tensor(name, shape, dt))

        def psum(name, shape):
            return ctx.enter_context(nc.psum_tensor(name, shape, F32))

        def sem(name):
            return ctx.enter_context(nc.semaphore(name))

        ident = sb("e_ident", [P, P])
        slot = sb("slot", [P, 2])
        row0 = sb("row0", [P, E])
        tile_ends = sb("tile_ends", [P, E, NTILE])
        at_most = sb("at_most", [P, E, NTILE], BF16)
        counts = sb("counts", [P, E, P])
        at_most_in_tile = sb("at_most_in_tile", [P, NRING, P], BF16)
        tiles = sb("tiles", [P, E])
        tile_c = sb("tile_c", [P, E])
        rowf = sb("rowf", [P, E])
        rows = sb("rows", [P, E], I32)
        within = sb("within", [P, E])
        tokf = sb("tokf", [P, E])
        tok_all = sb("tok_all", [P, E], I32)
        tok_ok = sb("tok_ok", [P, E])
        toks = sb("toks", [P, E], I32)

        w_gu = sb("e_w_gu", [P, NRING, DC, 2 * IE])
        w_down = sb("e_w_down", [P, NRING, D])
        xw = sb("xw", [P, NRING, D + E])
        xT = sb("e_xT", [P, NRING, DC, P])
        silu = sb("e_silu", [P, NRING, P])
        act = sb("e_act", [P, NRING, P])
        y_e = sb("y_e", [P, NRING, D])

        ps_t = psum("ps_t", [P, 2, 512])
        ps_gu = psum("e_ps_gu", [P, 2, 512])
        ps_y = psum("ps_y", [P, 2, 512])

        waited = sem("e_waited")
        consts_in = sem("e_consts_in")
        ends_in = [sem("ends_in0"), sem("ends_in1")]
        compared = sem("compared")
        tiles_done = sem("tiles_done")
        tile_c_done = sem("tile_c_done")
        rowf_done = sem("rowf_done")
        rows_done = sem("rows_done")
        counts_in = sem("counts_in")
        compared_in_tile = sem("compared_in_tile")
        within_done = sem("within_done")
        tokf_done = sem("tokf_done")
        tok_ok_done = sem("tok_ok_done")
        toks_done = sem("toks_done")
        w_in = [sem(f"e_w_in{r}") for r in range(NRING)]
        x_in = [sem(f"e_x_in{r}") for r in range(NRING)]
        transposed = sem("e_transposed")
        xT_done = sem("e_xT_done")
        gu_done = sem("e_gu_done")
        silu_done = sem("e_silu_done")
        act_done = sem("e_act_done")
        down_done = sem("e_down_done")
        y_done = sem("e_y_done")
        added = sem("added")

        count_rows = cum_dram.rearrange("e (t p) -> (e t) p", p=P)
        gu_e = expert_gu_w.rearrange("e (c p) f -> e p c f", p=P)
        PARTS = (slice(0, FIRST), slice(FIRST, E))

        def per_expert(engine, step):
            for r in range(NRING):
                step(r, r, 0, True)
            with engine.Fori(1, NCHK) as i:
                for r in range(NRING):
                    step(i * NRING + r, r, i, False)

        with nc.Block() as block:
            @block.sync
            def _(sp):
                sp.dma_start(slot[:, :], consts[:, 2 * P:2 * P + 2]).then_inc(consts_in, 16)
                sp.dma_start(row0[:, :], consts[:, 3 * P:3 * P + E]).then_inc(consts_in, 16)
                for n, part in enumerate(PARTS):
                    sp.dma_start(tile_ends[:, part].rearrange("p e t -> p (e t)"),
                                 ends_dram[part].rearrange("e (t o) -> o (e t)", o=1).partition_broadcast(P)
                                 ).then_inc(ends_in[n], 16)
                sp.dma_start(ident[:, :], consts[:, 0:P]).then_inc(consts_in, 16)

                def load(e, r, i, early):
                    if not early:
                        sp.wait_ge(down_done, e - (NRING - 1))
                    sp.dma_start(w_gu[:, r], gu_e[e]).then_inc(w_in[r], 16)
                    sp.dma_start(w_down[:, r], expert_down_w[e]).then_inc(w_in[r], 16)
                per_expert(sp, load)

            @block.gpsimd
            def _(pool):
                def gather_counts(e):
                    if e % NRING == 0:
                        pool.wait_ge(rows_done, 1 if e < FIRST else 2)
                        if e:
                            pool.wait_ge(counts_in, 16 * e)
                    pool.indirect_dma_start(counts[:, e, :], None, count_rows,
                                            bass.IndirectOffsetOnAxis(rows[:, e:e + 1], 0)).then_inc(counts_in, 16)

                def gather(e):
                    r = e % NRING
                    if r == 0:
                        pool.wait_ge(toks_done, (e // NRING + 1) * 2)
                    if e >= NRING:
                        pool.wait_ge(y_done, e - NRING + 1)
                    pool.indirect_dma_start(xw[:, r, :], None, table_dram,
                                            bass.IndirectOffsetOnAxis(toks[:, e:e + 1], 0)).then_inc(x_in[r], 16)

                def scatter(e):
                    if e >= 1:
                        pool.wait_ge(added, 16 * e)
                    pool.wait_ge(y_done, e + 1)
                    pool.indirect_dma_start(y_dram, bass.IndirectOffsetOnAxis(tok_all[:, e:e + 1], 0), y_e[:, e % NRING, :],
                                            None, bounds_check=TOK - 1, oob_is_err=False,
                                            compute_op=ALU.add).then_inc(added, 16)

                for e in range(NRING):
                    gather_counts(e)
                for e in range(GATHERED):
                    gather(e)
                for e in range(NRING, 2 * NRING):
                    gather_counts(e)
                for e in range(E):
                    if e + GATHERED < E:
                        gather(e + GATHERED)
                    if e + 2 * NRING < E:
                        gather_counts(e + 2 * NRING)
                    scatter(e)
                pool.wait_ge(added, 16 * E)

            @block.scalar
            def _(act_e):
                def work(e, r, i, early):
                    if not early:
                        act_e.wait_ge(gu_done, e - (NRING - 1))
                    act_e.wait_ge(transposed, e + 1)
                    act_e.activation(xT[:, r].rearrange("p c t -> p (c t)"), ps_t[:, r % 2, 0:DC * P], ACT.Copy).then_inc(xT_done, 1)
                    if not early:
                        act_e.wait_ge(act_done, e - (NRING - 1))
                    act_e.wait_ge(gu_done, e + 1)
                    act_e.activation(silu[:, r], ps_gu[:, r % 2, 0:P], ACT.Silu).then_inc(silu_done, 1)
                per_expert(act_e, work)

            @block.vector
            def _(dve):
                def find_tiles(n):
                    part = PARTS[n]
                    dve.wait_ge(ends_in[n], 16)
                    dve.tensor_scalar(at_most[:, part], tile_ends[:, part], slot[:, 0:1], None,
                                      ALU.is_le).then_inc(compared, 1)
                    dve.wait_ge(compared, n + 1)
                    dve.tensor_reduce(tiles[:, part], at_most[:, part], AX_X, ALU.add).then_inc(tiles_done, 1)
                    dve.wait_ge(tiles_done, n + 1)
                    dve.tensor_scalar(tile_c[:, part], tiles[:, part], float(NTILE - 1), None, ALU.min).then_inc(tile_c_done, 1)
                    dve.wait_ge(tile_c_done, n + 1)
                    dve.tensor_tensor(rowf[:, part], tile_c[:, part], row0[:, part], ALU.add).then_inc(rowf_done, 1)
                    dve.wait_ge(rowf_done, n + 1)
                    dve.tensor_copy(rows[:, part], rowf[:, part]).then_inc(rows_done, 1)

                def find_tokens(i):
                    es = bass.ds(i * NRING, NRING)
                    if not isinstance(i, int) or i > 0:
                        dve.wait_ge(within_done, i)
                    dve.wait_ge(counts_in, (i + 1) * (16 * NRING))
                    dve.tensor_scalar(at_most_in_tile[:, :, :], counts[:, es], slot[:, 0:1], None,
                                      ALU.is_le).then_inc(compared_in_tile, 1)
                    dve.wait_ge(compared_in_tile, i + 1)
                    dve.tensor_reduce(within[:, es], at_most_in_tile[:, :, :], AX_X, ALU.add).then_inc(within_done, 1)
                    dve.wait_ge(within_done, i + 1)
                    dve.scalar_tensor_tensor(out=tokf[:, es], in0=tile_c[:, es], scalar=float(P), in1=within[:, es],
                                             op0=ALU.mult, op1=ALU.add).then_inc(tokf_done, 1)
                    dve.wait_ge(tokf_done, i + 1)
                    dve.tensor_scalar(tok_ok[:, es], tokf[:, es], float(TOK - 1), None, ALU.min).then_inc(tok_ok_done, 1)
                    dve.tensor_copy(tok_all[:, es], tokf[:, es]).then_inc(toks_done, 1)
                    dve.wait_ge(tok_ok_done, i + 1)
                    dve.tensor_copy(toks[:, es], tok_ok[:, es]).then_inc(toks_done, 1)

                def work(e, r, i, early):
                    if not early:
                        dve.wait_ge(down_done, e - (NRING - 1))
                    dve.wait_ge(silu_done, e + 1)
                    dve.tensor_tensor(act[:, r], silu[:, r], ps_gu[:, r % 2, P:2 * P], ALU.mult).then_inc(act_done, 1)

                def weigh(e, r, early):
                    if not early:
                        dve.wait_ge(added, (e - (NRING - 1)) * 16)
                    dve.wait_ge(down_done, e + 1)
                    dve.tensor_scalar(y_e[:, r], ps_y[:, r % 2, 0:D], xw[:, r, bass.ds(e + D, 1)],
                                      None, ALU.mult).then_inc(y_done, 1)

                dve.wait_ge(consts_in, 48)
                find_tiles(0)
                find_tokens(0)
                find_tiles(1)
                for r in range(NRING):
                    work(r, r, 0, True)
                    if r > 0:
                        weigh(r - 1, r - 1, True)
                    if r == 1:
                        find_tokens(1)
                with dve.Fori(1, NCHK - 1) as i:
                    for r in range(NRING):
                        work(i * NRING + r, r, i, False)
                        weigh(i * NRING + (r - 1), (r - 1) % NRING, False)
                        if r == 1:
                            find_tokens(i + 1)
                for e in range(E - NRING, E):
                    work(e, e % NRING, NCHK - 1, False)
                    weigh(e - 1, (e - 1) % NRING, False)
                weigh(E - 1, NRING - 1, False)

            @block.tensor
            def _(pe):
                pe.wait_ge(consts_in, 48)

                def up(e, r, i, early):
                    if not (early and r < 2):
                        pe.wait_ge(xT_done, e - 1)
                    pe.wait_ge(x_in[r], i * 16 + 16)
                    for c in range(DC):
                        last = pe.transpose(ps_t[:, r % 2, c * P:(c + 1) * P], xw[:, r, c * P:(c + 1) * P], ident[:, :])
                    last.then_inc(transposed, 1)
                    if not (early and r < 2):
                        pe.wait_ge(act_done, e - 1)
                    pe.wait_ge(w_in[r], i * 32 + 32)
                    pe.wait_ge(xT_done, e + 1)
                    for k in range(2):
                        for c in range(DC):
                            last = pe.matmul(ps_gu[:, r % 2, k * P:(k + 1) * P], w_gu[:, r, c, k * IE:(k + 1) * IE],
                                             xT[:, r, c, :], start=(c == 0), stop=(c == DC - 1))
                    last.then_inc(gu_done, 1)

                def down(e, r, early):
                    if not (early and r < 2):
                        pe.wait_ge(y_done, e - 1)
                    pe.wait_ge(act_done, e + 1)
                    pe.matmul(ps_y[:, r % 2, 0:D], act[:, r], w_down[:, r], start=True, stop=True).then_inc(down_done, 1)

                for r in range(NRING):
                    up(r, r, 0, True)
                    if r > 0:
                        down(r - 1, r - 1, True)
                with pe.Fori(1, NCHK) as i:
                    for r in range(NRING):
                        up(i * NRING + r, r, i, False)
                        down(i * NRING + (r - 1), (r - 1) % NRING, False)
                down(E - 1, NRING - 1, False)


H, HD = 16, 16
GH = 4
NG = H // GH
GD = GH * HD
QT = S // P
HALF = 512
TERMS_Q = (0, 1, 0, 2, 0, 1)
TERMS_K = (0, 0, 1, 0, 2, 1)
NT = len(TERMS_Q) * HD
NPART = 3
UNITS = [(0, kt) for kt in (0, 3, 2, 1)] + [(1, kt) for kt in (0, 7, 6, 5, 4, 1, 2, 3)]
CHUNKS = [(qt, kh) for qt in range(QT) for kh in range(qt // 4 + 1)]
NU = len(UNITS)
NCH = GH * len(CHUNKS)
AHEAD = 3
UNIT_CHUNKS = (8, 3, 6, 4, 9, 4, 4, 5, 5)
TURN_UNIT = 9
POOL_TERMS = (5,)


def attention(nc, x, w_qkv, w_proj, b_proj, consts, rope, xnT_dram, y_dram, out):
    with ExitStack() as ctx:
        def sb(name, shape, dt=F32):
            return ctx.enter_context(nc.sbuf_tensor(name, shape, dt))

        def psum(name, shape, dt=F32):
            return ctx.enter_context(nc.psum_tensor(name, shape, dt))

        def sem(name):
            return ctx.enter_context(nc.semaphore("a_" + name))

        const_f = sb("const_f", [P, 3, P])
        ident = sb("ident_bf", [P, P], BF16)
        mask_qk = sb("mask_qk", [P, P], BF16)
        mask_kq = sb("mask_kq", [P, P], BF16)
        cos = sb("cos", [P, S])
        sin = sb("sin", [P, S])
        w_qk = sb("w_qk", [P, DC, NG, 2 * GD])
        w_v = sb("w_v", [P, DC, D])
        w_o = sb("w_o", [P, DC, D])
        bias = sb("bias", [P, 1, D])
        xT = sb("xT", [P, 2, DC, BLK])
        qk = sb("qk", [P, 2, HALF])
        rot = sb("rot", [P, 2, HALF])
        qc = sb("qc", [P, 2, HALF])
        rs = sb("rs", [P, 2, HALF])
        parts = [sb(f"part{j}", [P, 2, HALF], BF16) for j in range(NPART)]
        qs = [sb(f"qs{g}", [P, GH, S], BF16) for g in range(NG)]
        ks = [sb(f"ks{g}", [P, GH, S], BF16) for g in range(NG)]
        v = [sb(f"v{g}", [P, QT, GH, 2 * HD]) for g in range(NG)]
        mx = sb("mx", [P, 2, GH, QT])
        m_rest = sb("m_rest", [P, GH, QT])
        m_parts = sb("m_parts", [P, NPART, GH, QT], BF16)
        m_rows = sb("m_rows", [NPART * GH * QT, P], BF16)
        probs = sb("probs", [P, 2, GH, HALF])
        o_sum = sb("o_sum", [P, 2, HALF])
        o_turned = sb("o_turned", [P, 2, HALF])
        o_inv = sb("o_inv", [P, 2, HALF // 32, 1])
        o_norm = sb("o_norm", [P, 2, HALF])
        oT = sb("oT", [P, DC, S])
        x_d = sb("x_d", [P, 4, 2, D])
        y_d = sb("y_d", [P, 4, 2, D])
        gate = sb("gate", [P, 4, 2, D])
        s_d = sb("s_d", [P, 2, 2, D])
        g_d = sb("g_d", [P, 2, 2, D])
        out_d = sb("out_d", [P, 2, 2, D])

        ps_s = psum("ps_s", [P, GH, HALF])
        ps_m = psum("ps_m", [P, 2, HALF])
        ps_o = psum("ps_o", [P, HALF])
        ps_x = psum("ps_x", [P, HALF])

        consts_in, made, cleared = sem("consts_in"), sem("made"), sem("cleared")
        waited = sem("waited")
        xT_in = sem("xT_in")
        qk_ps, qk_done, rot_done = sem("qk_ps"), sem("qk_done"), sem("rot_done")
        qc_done, rs_done, roped, high_done = sem("qc_done"), sem("rs_done"), sem("roped"), sem("high_done")
        rest_done, mid_done, low_done = sem("rest_done"), sem("mid_done"), sem("low_done")
        stacked = [sem(f"stacked{g}") for g in range(NG)]
        pool_stacked = [sem(f"pool_stacked{g}") for g in range(NG)]
        v_ps, v_done = sem("v_ps"), sem("v_done")
        mx_ps, mx_done, mx_all = sem("mx_ps"), sem("mx_done"), sem("mx_all")
        m1, m2, m3, m_split = sem("m1"), sem("m2"), sem("m3"), sem("m_split")
        mt_ps, m_rows_done = sem("mt_ps"), sem("m_rows_done")
        m_in = [sem(f"m_in{g}") for g in range(NG)]
        s_ps, p_done, pv_done = sem("s_ps"), sem("p_done"), sem("pv_done")
        o_done, turned_done, inv_done = sem("o_done"), sem("turned_done"), sem("inv_done")
        scaled_done, norm_done = sem("scaled_done"), sem("norm_done")
        o_in = [sem("o_in0"), sem("o_in1")]
        xd_in = [sem(f"xd_in{j}") for j in range(4)]
        pr_ps, pr_done, gate_done = sem("pr_ps"), sem("pr_done"), sem("gate_done")
        gated, out_done = sem("gated"), sem("out_done")
        out_sent = [sem("out_sent0"), sem("out_sent1")]

        ROTATE = [(r + HD // 2) % HD + r // HD * HD for r in range(32)]
        first_units = [UNITS.index((half, 0)) for half in range(2)]
        NSTACK = 16 * 2 * GH * (len(TERMS_Q) - len(POOL_TERMS))
        NSTACK_POOL = 16 * 2 * GH * len(POOL_TERMS)
        D_UNIT = {5: 0, 6: 1, 7: 2, 8: 3}

        def width(u):
            half, kt = UNITS[u]
            return min(HALF, S - kt * P) if half else HALF - kt * P

        def diagonal(u):
            half, kt = UNITS[u]
            return kt // 4 == half

        def unit_chunks(u):
            return range(sum(UNIT_CHUNKS[:u]), sum(UNIT_CHUNKS[:u + 1]))

        def per_batch(engine, body):
            body(0, True, False)
            with engine.Fori(1, B - 1) as b:
                body(b, False, False)
            body(B - 1, False, True)

        def target(b, g, ahead):
            t = g + ahead
            return b + t // NG, t % NG, b * NG + t

        with nc.Block() as block:
            @block.sync
            def _(sp):
                sp.dma_start(const_f[:, 0, :], consts[:, 0:P]).then_inc(consts_in, 16)
                sp.dma_start(const_f[:, 1:3, :].rearrange("p a b -> p (a b)"), rope[:, 2 * S:2 * S + 2 * P]).then_inc(consts_in, 16)
                sp.dma_start(cos[:, :], rope[:, 0:S]).then_inc(consts_in, 16)
                sp.dma_start(sin[:, :], rope[:, S:2 * S]).then_inc(consts_in, 16)
                wq = w_qkv.rearrange("(c p) n -> p c n", p=P)
                for k in range(2):
                    for c in range(DC):
                        sp.dma_start(w_qk[:, c, :, k * GD:(k + 1) * GD],
                                     wq[:, c, k * D:(k + 1) * D].rearrange("p (g d) -> p g d", g=NG)).then_inc(consts_in, 16)
                sp.dma_start(w_v[:, :, :], wq[:, :, 2 * D:3 * D]).then_inc(consts_in, 16)
                sp.dma_start(w_o[:, :, :], w_proj.rearrange("(c p) n -> p c n", p=P)).then_inc(consts_in, 16)
                sp.dma_start(bias[:, 0, :], b_proj.partition_broadcast(P)).then_inc(consts_in, 16)

                def load_xT(b):
                    sp.dma_start(xT[:, 0], xnT_dram[b * 2]).then_inc(xT_in, 16)
                    sp.dma_start(xT[:, 1], xnT_dram[b * 2 + 1]).then_inc(xT_in, 16)

                def stack(g, q):
                    if not isinstance(q, int) or q >= NG:
                        sp.wait_ge(s_ps, (q - (NG - 1)) * NU * GH)
                    sp.wait_ge(low_done, q * 2 + 2)
                    for h in range(GH):
                        for t in range(len(TERMS_Q)):
                            if t not in POOL_TERMS:
                                r = slice(t * HD, (t + 1) * HD)
                                sp.dma_start(qs[g][r, h, :], parts[TERMS_Q[t]][h * HD:(h + 1) * HD]
                                             .rearrange("p a n -> p (a n)")).then_inc(stacked[g], 16)
                                sp.dma_start(ks[g][r, h, :], parts[TERMS_K[t]][GD + h * HD:GD + (h + 1) * HD]
                                             .rearrange("p a n -> p (a n)")).then_inc(stacked[g], 16)

                def send(b, j):
                    sp.wait_ge(out_done, b * 4 + (j + 1))
                    sp.dma_start(out[bass.ds(b * S + j * 2 * P, 2 * P)].rearrange("(t p) d -> p t d", p=P),
                                   out_d[:, j % 2]).then_inc(out_sent[j % 2], 16)

                load_xT(0)
                for q in range(AHEAD):
                    stack(q, q)

                def body(b, first, last):
                    for g in range(NG):
                        q = b * NG + g
                        if g == 0 and not last:
                            sp.wait_ge(v_ps, q + NG)
                            load_xT(b + 1)
                        if g == 3:
                            if not first:
                                sp.wait_ge(out_done, b * 4)
                            for j in range(4):
                                tok = bass.ds(b * S + j * 2 * P, 2 * P)
                                sp.dma_start(x_d[:, j], x[tok].rearrange("(t p) d -> p t d", p=P)).then_inc(xd_in[j], 16)
                                sp.dma_start(y_d[:, j], y_dram[tok].rearrange("(t p) d -> p t d", p=P)).then_inc(xd_in[j], 16)
                        if g == 0 and not first:
                            for j in range(4):
                                send(b - 1, j)
                        if not (last and g >= NG - AHEAD):
                            tb, tg, tq = target(b, g, AHEAD)
                            stack(tg, tq)
                per_batch(sp, body)
                for j in range(4):
                    send(B - 1, j)
                for j in range(2):
                    sp.wait_ge(out_sent[j], 16 * 2 * B)

            @block.gpsimd
            def _(pool):
                for g in range(NG):
                    if g > 0:
                        pool.wait_ge(cleared, 2 * g)
                    pool.memset(v[g][:, :, :, HD:2 * HD], 1.0).then_inc(cleared, 1)
                    pool.wait_ge(cleared, 2 * g + 1)
                    pool.memset(ks[g][NT:NT + 32], 1.0).then_inc(cleared, 1)
                pool.wait_ge(cleared, 2 * NG)
                pool.wait_ge(consts_in, 16 * 11)

                def rope_split(g, q):
                    a = q * 2
                    for n in range(2):
                        pool.wait_ge(qk_done, a + (n + 1))
                        if not isinstance(q, int) or q >= 1:
                            pool.wait_ge(low_done, a + (n - 1))
                        pool.sem_inc(waited, 1)
                        pool.tensor_tensor(qc[:, n], qk[:, n], cos[:, n * HALF:(n + 1) * HALF], ALU.mult).then_inc(qc_done, 1)
                        pool.wait_ge(rot_done, a + (n + 1))
                        pool.sem_inc(waited, 1)
                        pool.tensor_tensor(rs[:, n], rot[:, n], sin[:, n * HALF:(n + 1) * HALF], ALU.mult).then_inc(rs_done, 1)
                        pool.wait_ge(qc_done, a + (n + 1))
                        pool.wait_ge(rs_done, a + (n + 1))
                        pool.sem_inc(waited, 1)
                        pool.tensor_tensor(qc[:, n], qc[:, n], rs[:, n], ALU.add).then_inc(roped, 1)
                    for n in range(2):
                        pool.wait_ge(high_done, a + (n + 1))
                        pool.wait_ge(roped, a + (n + 1))
                        pool.sem_inc(waited, 1)
                        pool.tensor_tensor(rs[:, n], qc[:, n], parts[0][:, n], ALU.subtract).then_inc(rest_done, 1)
                    for n in range(2):
                        pool.wait_ge(mid_done, a + (n + 1))
                        pool.wait_ge(rest_done, a + (n + 1))
                        pool.sem_inc(waited, 1)
                        pool.tensor_tensor(parts[2][:, n], rs[:, n], parts[1][:, n], ALU.subtract).then_inc(low_done, 1)
                    if not isinstance(q, int) or q >= NG:
                        pool.wait_ge(s_ps, (q - (NG - 1)) * NU * GH)
                    pool.wait_ge(low_done, a + 2)
                    pool.sem_inc(waited, 1)
                    for h in range(GH):
                        for t in POOL_TERMS:
                            r = slice(t * HD, (t + 1) * HD)
                            pool.dma_start(qs[g][r, h, :], parts[TERMS_Q[t]][h * HD:(h + 1) * HD]
                                           .rearrange("p a n -> p (a n)")).then_inc(pool_stacked[g], 16)
                            pool.dma_start(ks[g][r, h, :], parts[TERMS_K[t]][GD + h * HD:GD + (h + 1) * HD]
                                           .rearrange("p a n -> p (a n)")).then_inc(pool_stacked[g], 16)

                def move_heads(g, q, half):
                    pool.wait_ge(norm_done, q * 2 + (half + 1))
                    pool.sem_inc(waited, 1)
                    for h in range(GH):
                        r = (g % 2) * GD + h * HD
                        pool.dma_start(oT[r:r + HD, g // 2, half * HALF:(half + 1) * HALF],
                                       o_norm[32 * h:32 * h + HD, half]).then_inc(o_in[half], 16)

                for q in range(AHEAD):
                    rope_split(q, q)

                def body(b, first, last):
                    for g in range(NG):
                        q = b * NG + g
                        if g == 0 and not first:
                            move_heads(NG - 1, q - 1, 1)
                        if not (last and g >= NG - AHEAD):
                            tb, tg, tq = target(b, g, AHEAD)
                            rope_split(tg, tq)
                        if g > 0:
                            move_heads(g - 1, q - 1, 1)
                        if g == 0 and not first:
                            pool.wait_ge(pr_ps, b * 4)
                        move_heads(g, q, 0)
                per_batch(pool, body)
                move_heads(NG - 1, B * NG - 1, 1)

            @block.scalar
            def _(act):
                act.wait_ge(consts_in, 16 * 11)

                def qk_out(q, n):
                    if not isinstance(q, int) or q >= 1:
                        act.wait_ge(qc_done, q * 2 + (n - 1))
                        act.wait_ge(rot_done, q * 2 + (n - 1))
                    act.wait_ge(qk_ps, q * 2 + (n + 1))
                    act.activation(qk[:, n], ps_x[:, :], ACT.Copy).then_inc(qk_done, 1)

                def v_out(g, q):
                    if not isinstance(q, int) or q >= NG:
                        act.wait_ge(pv_done, (q - (NG - 1)) * NU)
                    act.wait_ge(v_ps, q + 1)
                    act.activation(v[g][:, :, :, 0:HD], ps_x[:, :].rearrange("p (t h d) -> p t h d", t=QT, h=GH),
                                   ACT.Copy).then_inc(v_done, 1)

                def high(g, q, n, stacked_before):
                    if n == 0 and stacked_before is not None:
                        act.wait_ge(stacked[(g - 1) % NG], stacked_before * NSTACK)
                        act.wait_ge(pool_stacked[(g - 1) % NG], stacked_before * NSTACK_POOL)
                    act.wait_ge(roped, q * 2 + (n + 1))
                    act.activation(parts[0][:, n], qc[:, n], ACT.Copy).then_inc(high_done, 1)

                def mid(q, n):
                    act.wait_ge(rest_done, q * 2 + (n + 1))
                    act.activation(parts[1][:, n], rs[:, n], ACT.Copy).then_inc(mid_done, 1)

                def max_rows(g, q):
                    if not isinstance(q, int) or q >= 1:
                        pg = (g - 1) % NG
                        act.wait_ge(m_in[pg], (q + (NG - 1 - pg)) // NG * 48 if isinstance(q, int) else
                                    (q - g) * 12 + (48 if g >= 1 else 0))
                    act.wait_ge(mt_ps, q + 1)
                    act.activation(m_rows[:, :], ps_x[0:NPART * GH * QT, 0:P // 2].bitcast(BF16), ACT.Copy).then_inc(m_rows_done, 1)
                    act.wait_ge(m_rows_done, q + 1)
                    for j in range(NPART):
                        act.dma_start(qs[g][NT + j:NT + j + 1].rearrange("o h (t n) -> o (h t) n", n=P),
                                      m_rows[j * GH * QT:(j + 1) * GH * QT]).then_inc(m_in[g], 16)

                def heads_out(q, half):
                    if not isinstance(q, int) or q >= 1:
                        act.wait_ge(norm_done, q * 2 + (half - 1))
                    act.wait_ge(pv_done, q * NU + (4 if half == 0 else NU))
                    act.activation(o_sum[:, half], ps_o[:, :], ACT.Copy).then_inc(o_done, 1)

                def gates(b):
                    for j in range(4):
                        act.wait_ge(xd_in[j], (b + 1) * 32)
                        act.activation(gate[:, j], y_d[:, j], ACT.Silu).then_inc(gate_done, 1)

                for q in range(AHEAD):
                    qk_out(q, 0)
                    qk_out(q, 1)
                    v_out(q, q)
                    high(q, q, 0, 1 if q else None)
                    high(q, q, 1, None)
                    mid(q, 0)
                    mid(q, 1)
                max_rows(0, 0)

                def body(b, first, last):
                    for g in range(NG):
                        q = b * NG + g
                        project = not (last and g >= NG - AHEAD)
                        tb, tg, tq = target(b, g, AHEAD)
                        for u in range(NU):
                            for h in range(GH):
                                if h == 0 and not (first and g == 0 and u < 2):
                                    act.wait_ge(pv_done, q * NU + (u - 1))
                                act.wait_ge(s_ps, q * NU * GH + (u * GH + h + 1))
                                w = width(u)
                                act.activation(probs[:, u % 2, h, 0:w], ps_s[:, h, 0:w], ACT.Exp,
                                               scale=HD ** -0.5).then_inc(p_done, 1)
                            if u == TURN_UNIT and not (last and g == NG - 1):
                                mb, mg, mq = target(b, g, 1)
                                max_rows(mg, mq)
                            if u == 0 and not (first and g == 0):
                                heads_out(q - 1, 1)
                            if u == 4:
                                heads_out(q, 0)
                            if project:
                                if u == 0:
                                    qk_out(tq, 0)
                                if u == 2:
                                    qk_out(tq, 1)
                                if u == 4:
                                    v_out(tg, tq)
                                if u == 5:
                                    pb, pg, _ = target(b, g, AHEAD - 1)
                                    high(tg, tq, 0, pb + 1)
                                if u == 6:
                                    high(tg, tq, 1, None)
                                if u == 8:
                                    mid(tq, 0)
                                if u == 9:
                                    mid(tq, 1)
                            if u == 3 and g == 0 and not first:
                                gates(b - 1)
                per_batch(act, body)
                heads_out(B * NG - 1, 1)
                gates(B - 1)

            @block.vector
            def _(dve):
                dve.wait_ge(consts_in, 16 * 11)
                for j, dst in enumerate((ident, mask_qk, mask_kq)):
                    dve.tensor_copy(dst[:, :], const_f[:, j, :]).then_inc(made, 1)

                def turn(q, n):
                    if not isinstance(q, int) or q >= 1:
                        dve.wait_ge(rs_done, q * 2 + (n - 1))
                    dve.wait_ge(qk_done, q * 2 + (n + 1))
                    dve.sem_inc(waited, 1)
                    dve.stream_shuffle(rot[:, n], qk[:, n], ROTATE).then_inc(rot_done, 1)

                def reduce(q, c):
                    h, (qt, kh) = c // len(CHUNKS), CHUNKS[c % len(CHUNKS)]
                    w = min(HALF, (qt + 1) * P - kh * HALF)
                    if c == 0 and (not isinstance(q, int) or q >= 1):
                        dve.wait_ge(m_split, q)
                    dve.wait_ge(mx_ps, q * NCH + (c + 1))
                    dve.tensor_reduce(mx[:, kh, h, qt:qt + 1], ps_m[:, c % 2, 0:w], AX_X, ALU.max).then_inc(mx_done, 1)

                def split_max(q):
                    dve.wait_ge(mx_done, (q + 1) * NCH)
                    dve.tensor_tensor(mx[:, 0, :, 4:QT], mx[:, 0, :, 4:QT], mx[:, 1, :, 4:QT], ALU.max).then_inc(mx_all, 1)
                    if not isinstance(q, int) or q >= 1:
                        dve.wait_ge(mt_ps, q)
                    dve.wait_ge(mx_all, q + 1)
                    dve.tensor_scalar(m_parts[:, 0], mx[:, 0], -1.0, None, ALU.mult).then_inc(m1, 1)
                    dve.wait_ge(m1, q + 1)
                    dve.scalar_tensor_tensor(out=m_rest[:, :, :], in0=mx[:, 0], scalar=-1.0, in1=m_parts[:, 0],
                                             op0=ALU.mult, op1=ALU.subtract).then_inc(m2, 1)
                    dve.wait_ge(m2, q + 1)
                    dve.tensor_copy(m_parts[:, 1], m_rest[:, :, :]).then_inc(m3, 1)
                    dve.wait_ge(m3, q + 1)
                    dve.tensor_tensor(m_parts[:, 2], m_rest[:, :, :], m_parts[:, 1], ALU.subtract).then_inc(m_split, 1)

                def normalise(b, g, q, half):
                    k = q * 2 + half
                    dve.wait_ge(o_done, k + 1)
                    dve.transpose(o_turned[:, half], o_sum[:, half]).then_inc(turned_done, 1)
                    blocks = o_turned[:, half].rearrange("p (t d) -> p t d", d=32)
                    dve.wait_ge(turned_done, k + 1)
                    dve.reciprocal(o_inv[:, half], blocks[:, :, HD:HD + 1]).then_inc(inv_done, 1)
                    dve.wait_ge(inv_done, k + 1)
                    dve.tensor_tensor(blocks[:, :, 0:HD], blocks[:, :, 0:HD],
                                      o_inv[:, half].to_broadcast([P, HALF // 32, HD]), ALU.mult).then_inc(scaled_done, 1)
                    if not isinstance(q, int) or q >= 1:
                        dve.wait_ge(o_in[half], q * 64)
                    dve.wait_ge(scaled_done, k + 1)
                    dve.transpose(o_norm[:, half], o_turned[:, half]).then_inc(norm_done, 1)

                def finish(b, j):
                    k = b * 4 + j
                    dve.wait_ge(pr_ps, k + 1)
                    dve.tensor_tensor(s_d[:, j % 2], ps_x[:, :].rearrange("p (t d) -> p t d", t=2),
                                      bias[:, :, :].to_broadcast([P, 2, D]), ALU.add).then_inc(pr_done, 1)
                    if j >= 2:
                        dve.wait_ge(out_done, b * 4 + (j - 1))
                    dve.wait_ge(gate_done, k + 1)
                    dve.wait_ge(pr_done, k + 1)
                    dve.tensor_tensor(g_d[:, j % 2], s_d[:, j % 2], gate[:, j], ALU.mult).then_inc(gated, 1)
                    if j >= 2:
                        dve.wait_ge(out_sent[j % 2], b * 32 + 16)
                    dve.wait_ge(gated, k + 1)
                    dve.tensor_tensor(out_d[:, j % 2], g_d[:, j % 2], x_d[:, j], ALU.add).then_inc(out_done, 1)

                for q in range(AHEAD):
                    turn(q, 0)
                    turn(q, 1)
                for c in range(NCH):
                    reduce(0, c)
                split_max(0)

                def body(b, first, last):
                    for g in range(NG):
                        q = b * NG + g
                        if g == NG - 1 and not first:
                            dve.wait_ge(out_sent[0], b * 32)
                            dve.wait_ge(out_sent[1], b * 32)
                        for u in range(NU):
                            if not (last and g == NG - 1):
                                for c in unit_chunks(u):
                                    reduce(q + 1, c)
                                if u == len(UNIT_CHUNKS) - 1:
                                    split_max(q + 1)
                            if u == 0 and not (last and g >= NG - AHEAD):
                                turn(target(b, g, AHEAD)[2], 0)
                            if u == 2 and not (last and g >= NG - AHEAD):
                                turn(target(b, g, AHEAD)[2], 1)
                            if u == (1 if g == 0 else TURN_UNIT) and not (first and g == 0):
                                normalise(b, (g - 1) % NG, q - 1, 1)
                            if u == TURN_UNIT:
                                normalise(b, g, q, 0)
                            if u in D_UNIT and g == 0 and not first:
                                finish(b - 1, D_UNIT[u])
                per_batch(dve, body)
                normalise(B, NG - 1, B * NG - 1, 1)
                for j in range(4):
                    finish(B - 1, j)

            @block.tensor
            def _(pe):
                pe.wait_ge(made, 3)
                pe.wait_ge(cleared, 2 * NG)
                pe.wait_ge(consts_in, 16 * 11)

                def project_qk(g, q, n, xT_count):
                    if n == 0:
                        if xT_count is not None:
                            pe.wait_ge(xT_in, xT_count)
                        if not isinstance(q, int) or q >= AHEAD:
                            pe.wait_ge(m_rows_done, q - AHEAD + 1)
                        elif q > 0:
                            pe.wait_ge(v_done, q)
                    else:
                        pe.wait_ge(qk_done, q * 2 + 1)
                    for c in range(DC):
                        last = pe.matmul(ps_x[:, :], w_qk[:, c, g, :], xT[:, n, c, :], start=(c == 0), stop=(c == DC - 1))
                        if c == DC - 1:
                            last.then_inc(qk_ps, 1)
                        yield

                def project_v(g, q):
                    pe.wait_ge(qk_done, q * 2 + 2)
                    for t in range(QT):
                        for c in range(DC):
                            last = pe.matmul(ps_x[:, t * GD:(t + 1) * GD], xT[:, t // 4, c, (t % 4) * P:(t % 4 + 1) * P],
                                             w_v[:, c, g * GD:(g + 1) * GD], start=(c == 0), stop=(c == DC - 1))
                        if t == QT - 1:
                            last.then_inc(v_ps, 1)
                        if t % 2:
                            yield

                def max_scores(g, q, c):
                    h, (qt, kh) = c // len(CHUNKS), CHUNKS[c % len(CHUNKS)]
                    w = min(HALF, (qt + 1) * P - kh * HALF)
                    diag = kh == qt // 4
                    if not (isinstance(q, int) and q == 0 and c < 2):
                        pe.wait_ge(mx_done, q * NCH + (c - 1))
                    last = pe.matmul(ps_m[:, c % 2, 0:w], qs[g][0:NT, h, qt * P:(qt + 1) * P],
                                     ks[g][0:NT, h, kh * HALF:kh * HALF + w], start=True, stop=not diag)
                    if diag:
                        last = pe.matmul(ps_m[:, c % 2, w - P:w], ident[:, :], mask_qk[:, :], start=False, stop=True)
                    last.then_inc(mx_ps, 1)

                def turn_max(q, before):
                    before()
                    pe.wait_ge(m_split, q + 1)
                    pe.transpose(ps_x[0:NPART * GH * QT, 0:P // 2].bitcast(BF16),
                                 m_parts[:, :, :, :].rearrange("p a h t -> p (a h t)"), ident[:, :]).then_inc(mt_ps, 1)

                def scores(g, q, u, h, free):
                    half, kt = UNITS[u]
                    w = width(u)
                    q0 = half * HALF + HALF - w
                    if free is not None:
                        pe.wait_ge(p_done, free)
                    last = pe.matmul(ps_s[:, h, 0:w], ks[g][0:NT + NPART, h, kt * P:(kt + 1) * P],
                                     qs[g][0:NT + NPART, h, q0:q0 + w], start=True, stop=not diagonal(u))
                    if diagonal(u):
                        last = pe.matmul(ps_s[:, h, 0:P], ident[:, :], mask_kq[:, :], start=False, stop=True)
                    last.then_inc(s_ps, 1)

                def values(g, q, u):
                    half, kt = UNITS[u]
                    w = width(u)
                    if u in first_units and not (isinstance(q, int) and q * 2 + half == 0):
                        pe.wait_ge(o_done, q * 2 + half)
                    pe.wait_ge(p_done, q * NU * GH + (u + 1) * GH)
                    for h in range(GH):
                        last = pe.matmul(ps_o[32 * h:32 * h + 32, HALF - w:HALF], v[g][:, kt, h, :], probs[:, u % 2, h, 0:w],
                                         start=u in first_units, stop=u + 1 in (first_units[1], NU), skip_group_check=True)
                    last.then_inc(pv_done, 1)

                def project_out(b, j, first_of_batch):
                    if j == 0:
                        pe.wait_ge(o_in[0], (b + 1) * 256)
                        pe.wait_ge(o_in[1], (b + 1) * 256)
                        first_of_batch()
                    else:
                        pe.wait_ge(pr_done, b * 4 + j)
                    for t in range(2):
                        for c in range(DC):
                            col = (2 * j + t) * P
                            last = pe.matmul(ps_x[:, t * D:(t + 1) * D], oT[:, c, col:col + P], w_o[:, c, :],
                                             start=(c == 0), stop=(c == DC - 1))
                    last.then_inc(pr_ps, 1)

                for q in range(AHEAD):
                    for part in (project_qk(q, q, 0, 32 if q == 0 else None), project_qk(q, q, 1, None), project_v(q, q)):
                        for _ in part:
                            pass
                pe.wait_ge(stacked[0], NSTACK)
                pe.wait_ge(pool_stacked[0], NSTACK_POOL)
                for c in range(NCH):
                    max_scores(0, 0, c)
                turn_max(0, lambda: pe.wait_ge(v_done, AHEAD))

                def body(b, first, last):
                    for g in range(NG):
                        q = b * NG + g
                        project = not (last and g >= NG - AHEAD)
                        tb, tg, tq = target(b, g, AHEAD)
                        nb, ng, nq = target(b, g, 1)
                        find_max = not (last and g == NG - 1)
                        for u in range(NU):
                            if u == 0:
                                pe.wait_ge(m_in[g], (b + 1) * 48)
                                if find_max:
                                    pe.wait_ge(stacked[ng], (nb + 1) * NSTACK)
                                    pe.wait_ge(pool_stacked[ng], (nb + 1) * NSTACK_POOL)
                            def pieces():
                                for h in range(GH):
                                    free = None if (first and g == 0 and u == 0) else q * NU * GH + ((u - 1) * GH + h + 1)
                                    scores(g, q, u, h, free)
                                    yield
                                if u == TURN_UNIT and find_max:
                                    def before():
                                        if g == 0 and not first:
                                            pe.wait_ge(pr_done, b * 4)
                                        elif project:
                                            pe.wait_ge(v_done, tq + 1)
                                        else:
                                            pe.wait_ge(m_rows_done, q + 1)
                                    turn_max(nq, before)
                                if project and u == 0:
                                    yield from project_qk(tg, tq, 0, (tb + 1) * 32 if tg == 0 else None)
                                if project and u == 2:
                                    yield from project_qk(tg, tq, 1, None)
                                if project and u == 4:
                                    yield from project_v(tg, tq)
                                if u in D_UNIT and g == 0 and not first:
                                    project_out(b - 1, D_UNIT[u], lambda: pe.wait_ge(v_done, tq + 1))
                                    yield
                                if u > 0:
                                    values(g, q, u - 1)
                                elif not (first and g == 0):
                                    values((g - 1) % NG, q - 1, NU - 1)
                                yield

                            chunks = list(unit_chunks(u)) if find_max else []
                            count = 4 + 1 + (project and u in (0, 2)) * DC + (project and u == 4) * QT // 2 + (
                                u in D_UNIT and g == 0 and not first)
                            for n, _ in enumerate(pieces()):
                                while chunks and (len(unit_chunks(u)) - len(chunks)) * count < (n + 1) * len(unit_chunks(u)):
                                    max_scores(ng, nq, chunks.pop(0))
                per_batch(pe, body)
                values(NG - 1, B * NG - 1, NU - 1)
                for j in range(4):
                    project_out(B - 1, j, lambda: pe.wait_ge(m_rows_done, B * NG))


def build(nc, x, w_qkv, w_proj, b_proj, gate_w, shared_gate_w, shared_gu_w, shared_down_w, expert_gu_w, expert_down_w,
          consts, rope, out):
    xnT_dram = nc.dram_tensor("xnT_dram", [NBLK, P, DC, BLK], F32).ap()
    cum_dram = nc.dram_tensor("cum_dram", [E, TOK], F32).ap()
    table_dram = nc.dram_tensor("table_dram", [TOK, D + E], F32).ap()
    ends_dram = nc.dram_tensor("ends_dram", [E, NTILE], F32).ap()
    y_dram = nc.dram_tensor("y_dram", [TOK, D], F32).ap()
    feed_forward(nc, x, gate_w, shared_gate_w, shared_gu_w, shared_down_w, expert_gu_w, expert_down_w,
                 consts, xnT_dram, y_dram, cum_dram, table_dram, ends_dram)
    experts(nc, expert_gu_w, expert_down_w, consts, y_dram, cum_dram, table_dram, ends_dram)
    attention(nc, x, w_qkv, w_proj, b_proj, consts, rope, xnT_dram, y_dram, out)


def constants():
    c = np.zeros((P, 3 * P + 2 * E), np.float32)
    c[:, 0:P] = np.eye(P)
    c[:, P:2 * P] = np.triu(np.ones((P, P)))
    c[:, 2 * P] = np.arange(P)
    c[:, 3 * P:3 * P + E] = P * np.arange(E)
    c[:, 3 * P + E:] = np.arange(E)
    return c


def rope_tables():
    inv_freq = (1.0 / 10000.0 ** (np.arange(0, HD, 2, dtype=np.float32) / np.float32(HD))).astype(np.float32)
    angle = (np.arange(S, dtype=np.float32)[:, None] * inv_freq[None, :]).astype(np.float32)
    cos, sin = np.cos(angle).T, np.sin(angle).T
    r = np.zeros((P, 2 * S + 2 * P), np.float32)
    r[:, 0:S] = np.tile(np.concatenate([cos, cos]), (P // HD, 1))
    r[:, S:2 * S] = np.tile(np.concatenate([-sin, sin]), (P // HD, 1))
    later = np.triu(np.ones((P, P), np.float32), 1) * MASKED
    r[:, 2 * S:2 * S + P] = later
    r[:, 2 * S + P:] = later.T
    return r


_INS = ['L0_attn_x', 'L0_attn_w_qkv', 'L0_attn_w_proj', 'L0_attn_b_proj', 'L0_ffn_gate_w', 'L0_ffn_shared_gate_w',
        'L0_ffn_shared_gate_up_w', 'L0_ffn_shared_down_w', 'L0_ffn_expert_gate_up_w', 'L0_ffn_expert_down_w']


def kernel(**inputs):
    import numpy as _np
    import concourse.bacc as _bacc
    from concourse import mybir as _mybir
    from concourse.bass_utils import run_bass_kernel_spmd as _run

    nc = _bacc.Bacc("TRN2", target_bir_lowering=False, num_devices=1)
    arrays, args = {}, []
    layouts = {name: _np.asarray(inputs[name]) for name in _INS}
    layouts['L0_attn_x'] = layouts['L0_attn_x'].reshape(TOK, D)
    layouts['constants'] = constants()
    layouts['rope'] = rope_tables()
    for name, a in layouts.items():
        a = _np.ascontiguousarray(a)
        arrays[f"in_{name}_dram"] = a
        args.append(nc.dram_tensor(f"in_{name}_dram", a.shape, _mybir.dt.from_np(a.dtype), kind="ExternalInput").ap())
    args.append(nc.dram_tensor("out_0_dram", (TOK, D), _mybir.dt.float32, kind="ExternalOutput").ap())
    build(nc, *args)
    r = _run(nc, [arrays], core_ids=[0])
    return r.results[0]["out_0_dram"].reshape(B, S, D)
```
